# Optimizing a Trainium2 kernel written in Bass

```python
import numpy as np
import jax
import jax.numpy as jnp

def _softmax(x, axis=-1):
    return jax.nn.softmax(x, axis=axis)

def _gelu(x):
    return jax.nn.gelu(x, approximate=True)

def _silu(x):
    return jax.nn.silu(x)

def _sigmoid(x):
    return jax.nn.sigmoid(x)

def _layernorm(x, axis=-1, eps=1e-05):
    m = jnp.mean(x, axis=axis, keepdims=True)
    v = jnp.var(x, axis=axis, keepdims=True)
    return (x - m) / jnp.sqrt(v + eps)

def _scatter_add(tgt, idx, src, axis=0):
    return tgt.at[idx].add(src)

def _segment_sum(src, seg, n):
    return jax.ops.segment_sum(src, seg, n)
kernel_name = 'mk_perceiver_d1_seqx_r4_abe5f5'

def setup_inputs(seed: int=0):
    np.random.seed(seed)
    _w = jnp.asarray

    def _rec_inputs():
        import jax
        import jax.numpy as jnp
        _rk = jax.random.key(seed)
        x = 7.22e-05 + 1 * jax.random.normal(jax.random.fold_in(_rk, 1), (1, 128, 256), jnp.float32)
        _lenS = 128 - jax.random.randint(jax.random.fold_in(_rk, 7), (1,), 0, max(1, 128 // 4) + 1, jnp.int32)
        _lenS2 = 12544 - jax.random.randint(jax.random.fold_in(_rk, 8), (1,), 0, max(1, 12544 // 4) + 1, jnp.int32)
        _ctx_1024P = jax.random.normal(jax.random.fold_in(_rk, 11), (1, 16, 256), jnp.float32)
        _ctx_1024c = jax.random.dirichlet(jax.random.fold_in(_rk, 511), 0.3 * jnp.ones((16,), jnp.float32), (1, 12544))
        _ctx_1024t = jnp.einsum('bsk,bkd->bsd', _ctx_1024c, _ctx_1024P)
        _ctx_1024t = _ctx_1024t * jax.lax.rsqrt(jnp.mean(jnp.square(_ctx_1024t)) + 1e-12) * 0.953939
        ctx_1024 = 4.13588e-05 + 0.999923 * (_ctx_1024t + 0.3 * jax.random.normal(jax.random.fold_in(_rk, 611), (1, 12544, 256), jnp.float32))
        return (x, ctx_1024)
    x, ctx_1024 = _rec_inputs()

    def _L0_xattn_setup():
        import jax, jax.numpy as jnp
        import numpy as np
        D_MODEL = 256
        N_HEADS = 16
        D_K = D_MODEL // N_HEADS
        B, S = (4, 512)

        def _xavier(key, out_dim, in_dim):
            limit = float(np.sqrt(6.0 / (in_dim + out_dim)))
            return jax.random.uniform(key, (out_dim, in_dim), jnp.float32, -limit, limit)
        key = jax.random.key(seed)
        ks = jax.random.split(key, 7)
        return {'query': jax.random.normal(ks[0], (B, S, D_MODEL), jnp.float32), 'key': jax.random.normal(ks[1], (B, S, D_MODEL), jnp.float32), 'value': jax.random.normal(ks[2], (B, S, D_MODEL), jnp.float32), 'W_q': _xavier(ks[3], D_MODEL, D_MODEL), 'b_q': jnp.zeros((D_MODEL,), jnp.float32), 'W_k': _xavier(ks[4], D_MODEL, D_MODEL), 'b_k': jnp.zeros((D_MODEL,), jnp.float32), 'W_v': _xavier(ks[5], D_MODEL, D_MODEL), 'b_v': jnp.zeros((D_MODEL,), jnp.float32), 'W_o': _xavier(ks[6], D_MODEL, D_MODEL), 'b_o': jnp.zeros((D_MODEL,), jnp.float32)}
    _L0_xattn_all = _L0_xattn_setup()
    _L0_xattn_in = {k: v for k, v in _L0_xattn_all.items() if k in ('W_q', 'b_q', 'W_k', 'b_k', 'W_v', 'b_v', 'W_o', 'b_o')}
    del _L0_xattn_all

    def _L0_attn_setup():
        import jax, jax.numpy as jnp
        import numpy as np
        import math
        DIM = 256
        DIM_HEAD = 64
        HEADS = 16
        B, N = (2, 512)

        def _layernorm(x, g, b, eps=1e-05):
            x32 = x.astype(jnp.float32)
            mu = jnp.mean(x32, axis=-1, keepdims=True)
            var = jnp.var(x32, axis=-1, keepdims=True)
            return ((x32 - mu) * jax.lax.rsqrt(var + eps) * g + b).astype(x.dtype)
        key = jax.random.key(seed)
        ks = jax.random.split(key, 8)
        inner = DIM_HEAD * HEADS
        return {'x': jax.random.normal(ks[0], (B, N, DIM), dtype=jnp.float32), 'w_q': jax.random.normal(ks[1], (inner, DIM), dtype=jnp.float32) * 0.02, 'w_kv': jax.random.normal(ks[2], (2 * DIM_HEAD, DIM), dtype=jnp.float32) * 0.02, 'w_out': jax.random.normal(ks[3], (DIM, inner), dtype=jnp.float32) * 0.02, 'ln_g': jnp.ones((DIM,), dtype=jnp.float32), 'ln_b': jnp.zeros((DIM,), dtype=jnp.float32), 'lno_g': jnp.ones((DIM,), dtype=jnp.float32), 'lno_b': jnp.zeros((DIM,), dtype=jnp.float32)}
    _L0_attn_all = _L0_attn_setup()
    _L0_attn_in = {k: v for k, v in _L0_attn_all.items() if k in ('w_q', 'w_kv', 'w_out', 'ln_g', 'ln_b', 'lno_g', 'lno_b')}
    del _L0_attn_all

    def _L0_ffn_setup():
        import jax, jax.numpy as jnp
        import numpy as np
        DIM = 256
        DEPTH = 6
        HEADS = 16
        DIM_HEAD = 64
        WINDOW = 64
        INNER = HEADS * DIM_HEAD
        DIM_INNER = int(DIM * 4 * 2 / 3)
        QK_SCALE = 8.0

        def shift_tokens(t):
            a, s = jnp.split(t, 2, -1)
            s = jnp.pad(s, ((0, 0), (1, 0), (0, 0)))[:, :-1]
            return jnp.concatenate([a, s], -1)

        def l2norm(t):
            return t / jnp.maximum(jnp.linalg.norm(t, axis=-1, keepdims=True), 1e-12)

        def rotate_half(x):
            x1, x2 = jnp.split(x, 2, -1)
            return jnp.concatenate([-x2, x1], -1)

        def rotary_tables(n):
            half = jnp.arange(0, DIM_HEAD, 2, dtype=jnp.float32)
            inv_freq = 1.0 / 10000.0 ** (half / DIM_HEAD)
            t = jnp.arange(n, dtype=jnp.float32)
            freqs = t[:, None] * inv_freq[None, :]
            freqs = jnp.concatenate([freqs, freqs], -1)
            base_scale = (half + 0.4 * DIM_HEAD) / (1.4 * DIM_HEAD)
            power = (t - n // 2) / (WINDOW // 2)
            scale = base_scale[None, :] ** power[:, None]
            scale = jnp.concatenate([scale, scale], -1)
            return (freqs, scale)

        def local_attention(q, k, v):
            b, h, n, d = q.shape
            w = WINDOW
            nw = n // w
            bq = q.reshape(b, h, nw, w, d)
            bk = k.reshape(b, h, nw, w, d)
            bv = v.reshape(b, h, nw, w, d)

            def look(t):
                p = jnp.pad(t, ((0, 0), (0, 0), (1, 0), (0, 0), (0, 0)))
                return jnp.concatenate([p[:, :, :nw], p[:, :, 1:]], axis=3)
            bk2, bv2 = (look(bk), look(bv))
            seq = jnp.arange(n).reshape(nw, w)
            seq_p = jnp.pad(seq, ((1, 0), (0, 0)), constant_values=-1)
            jt = jnp.concatenate([seq_p[:nw], seq_p[1:]], axis=1)
            it = seq[:, :, None]
            jb = jt[:, None, :]
            mask = (it < jb) | (it > jb + w) | (jb == -1)
            sim = jnp.einsum('bhwie,bhwje->bhwij', bq, bk2) * QK_SCALE
            sim = jnp.where(mask, -jnp.finfo(sim.dtype).max, sim)
            attn = jax.nn.softmax(sim, -1)
            out = jnp.einsum('bhwij,bhwje->bhwie', attn, bv2)
            return out.reshape(b, h, n, d)

        def attn_layer(x, Wqkv, qs, ksc, Wo):
            b, n, _ = x.shape
            qkv = x @ Wqkv
            q, k, v = jnp.split(qkv, 3, -1)
            sh = lambda t: t.reshape(b, n, HEADS, DIM_HEAD).transpose(0, 2, 1, 3)
            q, k, v = (sh(q), sh(k), sh(v))
            q = l2norm(q) * qs
            k = l2norm(k) * ksc
            freqs, scale = rotary_tables(n)
            cos, sin = (jnp.cos(freqs), jnp.sin(freqs))
            q = q * cos * scale + rotate_half(q) * sin * scale
            inv = 1.0 / scale
            k = k * cos * inv + rotate_half(k) * sin * inv
            out = local_attention(q, k, v)
            out = out.transpose(0, 2, 1, 3).reshape(b, n, INNER)
            return out @ Wo

        def ffn_layer(x, g, bln, W1, b1, W2, b2):
            mu = x.mean(-1, keepdims=True)
            var = ((x - mu) ** 2).mean(-1, keepdims=True)
            xn = (x - mu) / jnp.sqrt(var + 1e-05) * g + bln
            hg = xn @ W1 + b1
            a, gate = jnp.split(hg, 2, -1)
            return a * jax.nn.gelu(gate, approximate=False) @ W2 + b2
        key = jax.random.key(seed)
        ks = jax.random.split(key, 8)
        B, N = (2, 512)
        init = lambda k, shape: jax.random.normal(k, shape, jnp.float32) * 0.02
        return {'x': jax.random.normal(ks[0], (B, N, DIM), jnp.float32), 'Wqkv': init(ks[1], (DEPTH, DIM, 3 * INNER)), 'q_scale': jnp.ones((DEPTH, DIM_HEAD), jnp.float32), 'k_scale': jnp.ones((DEPTH, DIM_HEAD), jnp.float32), 'Wo': init(ks[2], (DEPTH, INNER, DIM)), 'ln_g': jnp.ones((DEPTH, DIM), jnp.float32), 'ln_b': jnp.zeros((DEPTH, DIM), jnp.float32), 'W1': init(ks[3], (DEPTH, DIM, 2 * DIM_INNER)), 'b1': jnp.zeros((DEPTH, 2 * DIM_INNER), jnp.float32), 'W2': init(ks[4], (DEPTH, DIM_INNER, DIM)), 'b2': jnp.zeros((DEPTH, DIM), jnp.float32)}
    _L0_ffn_all = _L0_ffn_setup()
    _L0_ffn_in = {k: v for k, v in _L0_ffn_all.items() if k in ('Wqkv', 'q_scale', 'k_scale', 'Wo', 'ln_g', 'ln_b', 'W1', 'b1', 'W2', 'b2')}
    del _L0_ffn_all
    return {'x': x, 'ctx_1024': ctx_1024, 'L0_xattn_W_q': _L0_xattn_in['W_q'], 'L0_xattn_b_q': _L0_xattn_in['b_q'], 'L0_xattn_W_k': _L0_xattn_in['W_k'], 'L0_xattn_b_k': _L0_xattn_in['b_k'], 'L0_xattn_W_v': _L0_xattn_in['W_v'], 'L0_xattn_b_v': _L0_xattn_in['b_v'], 'L0_xattn_W_o': _L0_xattn_in['W_o'], 'L0_xattn_b_o': _L0_xattn_in['b_o'], 'L0_attn_w_q': _L0_attn_in['w_q'], 'L0_attn_w_kv': _L0_attn_in['w_kv'], 'L0_attn_w_out': _L0_attn_in['w_out'], 'L0_attn_ln_g': _L0_attn_in['ln_g'], 'L0_attn_ln_b': _L0_attn_in['ln_b'], 'L0_attn_lno_g': _L0_attn_in['lno_g'], 'L0_attn_lno_b': _L0_attn_in['lno_b'], 'L0_ffn_Wqkv': _L0_ffn_in['Wqkv'], 'L0_ffn_q_scale': _L0_ffn_in['q_scale'], 'L0_ffn_k_scale': _L0_ffn_in['k_scale'], 'L0_ffn_Wo': _L0_ffn_in['Wo'], 'L0_ffn_ln_g': _L0_ffn_in['ln_g'], 'L0_ffn_ln_b': _L0_ffn_in['ln_b'], 'L0_ffn_W1': _L0_ffn_in['W1'], 'L0_ffn_b1': _L0_ffn_in['b1'], 'L0_ffn_W2': _L0_ffn_in['W2'], 'L0_ffn_b2': _L0_ffn_in['b2']}

def reference(x, ctx_1024, L0_xattn_W_q, L0_xattn_b_q, L0_xattn_W_k, L0_xattn_b_k, L0_xattn_W_v, L0_xattn_b_v, L0_xattn_W_o, L0_xattn_b_o, L0_attn_w_q, L0_attn_w_kv, L0_attn_w_out, L0_attn_ln_g, L0_attn_ln_b, L0_attn_lno_g, L0_attn_lno_b, L0_ffn_Wqkv, L0_ffn_q_scale, L0_ffn_k_scale, L0_ffn_Wo, L0_ffn_ln_g, L0_ffn_ln_b, L0_ffn_W1, L0_ffn_b1, L0_ffn_W2, L0_ffn_b2):
    import jax
    import jax.numpy as jnp

    def _L0_xattn_ref(query, key, value, W_q, b_q, W_k, b_k, W_v, b_v, W_o, b_o):
        import jax, jax.numpy as jnp
        import numpy as np
        D_MODEL = 256
        N_HEADS = 16
        D_K = D_MODEL // N_HEADS
        B, S = (4, 512)

        def _xavier(key, out_dim, in_dim):
            limit = float(np.sqrt(6.0 / (in_dim + out_dim)))
            return jax.random.uniform(key, (out_dim, in_dim), jnp.float32, -limit, limit)
        b, sq, _ = query.shape
        sk = key.shape[1]
        Q = (query @ W_q.T + b_q).reshape(b, sq, N_HEADS, D_K).transpose(0, 2, 1, 3)
        K = (key @ W_k.T + b_k).reshape(b, sk, N_HEADS, D_K).transpose(0, 2, 1, 3)
        V = (value @ W_v.T + b_v).reshape(b, sk, N_HEADS, D_K).transpose(0, 2, 1, 3)
        scores = jnp.einsum('bhqd,bhkd->bhqk', Q, K) / jnp.sqrt(jnp.float32(D_K))
        attn = jax.nn.softmax(scores, axis=-1)
        out = jnp.einsum('bhqk,bhkd->bhqd', attn, V)
        out = out.transpose(0, 2, 1, 3).reshape(b, sq, D_MODEL)
        return out @ W_o.T + b_o

    def _L0_attn_ref(x, w_q, w_kv, w_out, ln_g, ln_b, lno_g, lno_b):
        import jax, jax.numpy as jnp
        import numpy as np
        import math
        DIM = 256
        DIM_HEAD = 64
        HEADS = 16
        B, N = (2, 512)

        def _layernorm(x, g, b, eps=1e-05):
            x32 = x.astype(jnp.float32)
            mu = jnp.mean(x32, axis=-1, keepdims=True)
            var = jnp.var(x32, axis=-1, keepdims=True)
            return ((x32 - mu) * jax.lax.rsqrt(var + eps) * g + b).astype(x.dtype)
        b, n, _ = x.shape
        scale = DIM_HEAD ** (-0.5)
        xn = _layernorm(x, ln_g, ln_b)
        q = jnp.einsum('bnc,ec->bne', xn, w_q)
        kv = jnp.einsum('bnc,ec->bne', xn, w_kv)
        k, v = jnp.split(kv, 2, axis=-1)
        q = q.reshape(b, n, HEADS, DIM_HEAD).transpose(0, 2, 1, 3)
        sqs = math.sqrt(scale)
        q = q * (scale * sqs)
        k = k * sqs
        sim = jnp.einsum('bhid,bjd->bhij', q, k)
        max_neg = -jnp.finfo(sim.dtype).max
        causal_mask = jnp.triu(jnp.ones((n, n), dtype=bool), k=1)
        sim = jnp.where(causal_mask, max_neg, sim)
        attn = jax.nn.softmax(sim.astype(jnp.float32), axis=-1).astype(sim.dtype)
        out = jnp.einsum('bhij,bjd->bhid', attn, v)
        out = out.transpose(0, 2, 1, 3).reshape(b, n, HEADS * DIM_HEAD)
        out = jnp.einsum('bne,ce->bnc', out, w_out)
        return _layernorm(out, lno_g, lno_b)

    def _L0_ffn_ref(x, Wqkv, q_scale, k_scale, Wo, ln_g, ln_b, W1, b1, W2, b2):
        import jax, jax.numpy as jnp
        import numpy as np
        DIM = 256
        DEPTH = 6
        HEADS = 16
        DIM_HEAD = 64
        WINDOW = 64
        INNER = HEADS * DIM_HEAD
        DIM_INNER = int(DIM * 4 * 2 / 3)
        QK_SCALE = 8.0

        def shift_tokens(t):
            a, s = jnp.split(t, 2, -1)
            s = jnp.pad(s, ((0, 0), (1, 0), (0, 0)))[:, :-1]
            return jnp.concatenate([a, s], -1)

        def l2norm(t):
            return t / jnp.maximum(jnp.linalg.norm(t, axis=-1, keepdims=True), 1e-12)

        def rotate_half(x):
            x1, x2 = jnp.split(x, 2, -1)
            return jnp.concatenate([-x2, x1], -1)

        def rotary_tables(n):
            half = jnp.arange(0, DIM_HEAD, 2, dtype=jnp.float32)
            inv_freq = 1.0 / 10000.0 ** (half / DIM_HEAD)
            t = jnp.arange(n, dtype=jnp.float32)
            freqs = t[:, None] * inv_freq[None, :]
            freqs = jnp.concatenate([freqs, freqs], -1)
            base_scale = (half + 0.4 * DIM_HEAD) / (1.4 * DIM_HEAD)
            power = (t - n // 2) / (WINDOW // 2)
            scale = base_scale[None, :] ** power[:, None]
            scale = jnp.concatenate([scale, scale], -1)
            return (freqs, scale)

        def local_attention(q, k, v):
            b, h, n, d = q.shape
            w = WINDOW
            nw = n // w
            bq = q.reshape(b, h, nw, w, d)
            bk = k.reshape(b, h, nw, w, d)
            bv = v.reshape(b, h, nw, w, d)

            def look(t):
                p = jnp.pad(t, ((0, 0), (0, 0), (1, 0), (0, 0), (0, 0)))
                return jnp.concatenate([p[:, :, :nw], p[:, :, 1:]], axis=3)
            bk2, bv2 = (look(bk), look(bv))
            seq = jnp.arange(n).reshape(nw, w)
            seq_p = jnp.pad(seq, ((1, 0), (0, 0)), constant_values=-1)
            jt = jnp.concatenate([seq_p[:nw], seq_p[1:]], axis=1)
            it = seq[:, :, None]
            jb = jt[:, None, :]
            mask = (it < jb) | (it > jb + w) | (jb == -1)
            sim = jnp.einsum('bhwie,bhwje->bhwij', bq, bk2) * QK_SCALE
            sim = jnp.where(mask, -jnp.finfo(sim.dtype).max, sim)
            attn = jax.nn.softmax(sim, -1)
            out = jnp.einsum('bhwij,bhwje->bhwie', attn, bv2)
            return out.reshape(b, h, n, d)

        def attn_layer(x, Wqkv, qs, ksc, Wo):
            b, n, _ = x.shape
            qkv = x @ Wqkv
            q, k, v = jnp.split(qkv, 3, -1)
            sh = lambda t: t.reshape(b, n, HEADS, DIM_HEAD).transpose(0, 2, 1, 3)
            q, k, v = (sh(q), sh(k), sh(v))
            q = l2norm(q) * qs
            k = l2norm(k) * ksc
            freqs, scale = rotary_tables(n)
            cos, sin = (jnp.cos(freqs), jnp.sin(freqs))
            q = q * cos * scale + rotate_half(q) * sin * scale
            inv = 1.0 / scale
            k = k * cos * inv + rotate_half(k) * sin * inv
            out = local_attention(q, k, v)
            out = out.transpose(0, 2, 1, 3).reshape(b, n, INNER)
            return out @ Wo

        def ffn_layer(x, g, bln, W1, b1, W2, b2):
            mu = x.mean(-1, keepdims=True)
            var = ((x - mu) ** 2).mean(-1, keepdims=True)
            xn = (x - mu) / jnp.sqrt(var + 1e-05) * g + bln
            hg = xn @ W1 + b1
            a, gate = jnp.split(hg, 2, -1)
            return a * jax.nn.gelu(gate, approximate=False) @ W2 + b2
        for i in range(DEPTH):
            x = attn_layer(shift_tokens(x), Wqkv[i], q_scale[i], k_scale[i], Wo[i]) + x
            x = ffn_layer(shift_tokens(x), ln_g[i], ln_b[i], W1[i], b1[i], W2[i], b2[i]) + x
        return x
    x = x + _L0_xattn_ref(_layernorm(x, axis=-1), ctx_1024, ctx_1024, L0_xattn_W_q, L0_xattn_b_q, L0_xattn_W_k, L0_xattn_b_k, L0_xattn_W_v, L0_xattn_b_v, L0_xattn_W_o, L0_xattn_b_o)
    x = x + _L0_attn_ref(_layernorm(x, axis=-1), L0_attn_w_q, L0_attn_w_kv, L0_attn_w_out, L0_attn_ln_g, L0_attn_ln_b, L0_attn_lno_g, L0_attn_lno_b)
    x = x + _L0_ffn_ref(_layernorm(x, axis=-1), L0_ffn_Wqkv, L0_ffn_q_scale, L0_ffn_k_scale, L0_ffn_Wo, L0_ffn_ln_g, L0_ffn_ln_b, L0_ffn_W1, L0_ffn_b1, L0_ffn_W2, L0_ffn_b2)
    return x

_drawn_inputs = setup_inputs


def setup_inputs(seed=0):
    import zlib

    import numpy as np

    out = dict(_drawn_inputs(seed))
    spreads = {'L0_xattn_b_q': (0.0, 0.325),
     'L0_xattn_b_k': (0.0, 0.8),
     'L0_xattn_b_v': (0.0, 0.1),
     'L0_xattn_b_o': (0.0, 0.1),
     'L0_attn_ln_g': (1.0, 0.2),
     'L0_attn_ln_b': (0.0, 0.1),
     'L0_attn_lno_g': (1.0, 0.2),
     'L0_attn_lno_b': (0.0, 0.1),
     'L0_ffn_q_scale': (1.0, 0.6),
     'L0_ffn_k_scale': (1.0, 0.6),
     'L0_ffn_ln_g': (1.0, 0.6),
     'L0_ffn_ln_b': (0.0, 0.8),
     'L0_ffn_b1': (0.0, 0.588),
     'L0_ffn_b2': (0.0, 0.1)}
    factors = {'L0_attn_w_q': 8.0}
    for name, (base, spread) in spreads.items():
        noise = np.random.default_rng([zlib.crc32(name.encode()), seed]).standard_normal(out[name].shape)
        drawn = base * np.exp(spread * noise) if base else spread * noise
        out[name] = jnp.asarray(drawn.astype(out[name].dtype))
    for name, factor in factors.items():
        out[name] = (out[name] * factor).astype(out[name].dtype)
    return out
```

```python
from contextlib import ExitStack

import concourse.bass as bass
import numpy as np
from concourse import mybir

F32 = mybir.dt.float32
BF16 = mybir.dt.bfloat16
I32 = mybir.dt.int32
ALU = mybir.AluOpType
ACT = mybir.ActivationFunctionType
AX_X = mybir.AxisListType.X

P = 128
D = 256
DB = D // P
S = 12544
XH, XD = 16, 16
HT = P // XD
XS = float(XD) ** -0.5
C1 = 448
N1 = S // C1
C2 = 128
N2 = S // C2
VW = XD + 1
H, HD = 16, 64
INNER = H * HD
HP = H // 2
FF = 682
FB = -(-FF // P)
FR = FF - (FB - 1) * P
DEPTH = 6
WINDOW = 64
MQA_SCALE = float(HD) ** -1.0
QK_SCALE = 8.0
EPS = 1e-5
MASKED = -1e30
NORM_FLOOR = 1e-12
NEWTON = 3
ROOT_GUESS = float(0x5F3759DF)

IDENT, SHIFT, HEADM, CAUSAL, BAND, COSQ, SINQ, COSK, SINK, CONSTS = np.cumsum(
    [0, P, P, HT, P, P, HD, HD, HD, HD]).tolist()
BQ, BK, LNG, LNB, FG, FBIAS, B1A, B1G, COLS = np.cumsum(
    [0, DB, DB, DB, DB, DB * DEPTH, DB * DEPTH, FB * DEPTH, FB * DEPTH]).tolist()
BV, BO, LOG, LOB, B2, QSC, KSC, ROWS = np.cumsum(
    [0, D, D, D, D, D * DEPTH, HD * DEPTH, HD * DEPTH]).tolist()


def constants():
    t = np.zeros((P, CONSTS), np.float32)
    i = np.arange(P)
    t[:, IDENT:IDENT + P] = np.eye(P)
    t[:, SHIFT:SHIFT + P] = np.eye(P, k=1)
    t[:, HEADM:HEADM + HT] = i[:, None] // XD == np.arange(HT)[None, :]
    q, k = i[:, None], i[None, :]
    t[:, CAUSAL:CAUSAL + P] = np.where(k > q, MASKED, 0.0)
    t[:, BAND:BAND + P] = np.where((k > q) | (q > k + WINDOW), MASKED, 0.0)
    half = np.arange(0, HD, 2, dtype=np.float32)
    freqs = i.astype(np.float32)[:, None] * (1.0 / 10000.0 ** (half / HD)).astype(np.float32)[None, :]
    base = (half + 0.4 * HD) / (1.4 * HD)
    power = (i - P // 2) / (WINDOW // 2)
    scale = (base[None, :].astype(np.float32) ** power[:, None].astype(np.float32)).astype(np.float32)
    cos, sin = np.cos(freqs), np.sin(freqs)
    for c0, s0, sc in ((COSQ, SINQ, scale), (COSK, SINK, 1.0 / scale)):
        t[:, c0:c0 + HD] = np.concatenate([cos * sc, cos * sc], 1)
        t[:, s0:s0 + HD] = np.concatenate([-sin * sc, sin * sc], 1)
    return t


def build(nc, x, ctxT, wqT, wkT, wvT, woT, aq, akv, ao, wqkv, wo, w1, w2, cols, rows, consts, out):
    with ExitStack() as ctx:
        def sb(name, shape, dt=F32):
            return ctx.enter_context(nc.sbuf_tensor(name, shape, dt))

        known = {}

        def sem(name):
            if name not in known:
                known[name] = ctx.enter_context(nc.semaphore(name))
            return known[name]

        ps = ctx.enter_context(nc.psum_tensor("ps", [P, 8, 512], F32))

        def banks(a, n, inner):
            return ps[:, a:a + n, :].rearrange("p b (g c) -> p (b g) c", c=inner)

        arena = sb("arena", [P, DB * S])
        keysT = arena[:].rearrange("p (t n) -> p t n", t=DB)
        place = [0]

        def view(n, c=None):
            v = arena[:, place[0]:place[0] + n]
            place[0] += n
            return v if c is None else v.rearrange("p (g c) -> p g c", c=c)

        wqkv_s = view(DB * 3 * INNER, 3 * INNER)
        wo_s = view(HP * D, D)
        w1_s = view(DB * 2 * FF, 2 * FF)
        w2_s = view(FB * D, D)
        qkv_s = view(3 * INNER, HD)
        rot = view(2 * INNER, HD)
        t1 = view(INNER, HD)
        t2 = view(INNER, HD)
        qkT = view(2 * HP * P, P)
        probs = view(H * P, P)
        uT = view(FB * P, P)
        assert place[0] <= DB * S

        qbd = sb("qbd", [P, DB, HT, P])
        qbd16 = sb("qbd16", [P, DB, HT, P], BF16)
        keys16 = sb("keys16", [P, 2, DB, C1], BF16)
        ctx1 = sb("ctx1", [P, 2, DB, C1])
        ctx2 = sb("ctx2", [P, 2, DB, C2])
        keyst = sb("keyst", [P, 2, DB, C2])
        shift = sb("shift", [P, XH * P])
        expd = sb("expd", [P, 2, XH * P])
        vaug = sb("vaug", [P, 2, XH, VW])
        maxpart = sb("maxpart", [P, N1, XH])
        xmax = sb("xmax", [P, XH])
        wx = sb("wx", [P, 4, DB, D])
        aq_s = sb("aq_s", [P, DB, INNER])
        akv_s = sb("akv_s", [P, DB, 2 * HD])
        ao_s = sb("ao_s", [P, HP, D])
        colv = sb("colv", [P, COLS])
        rowv = sb("rowv", [P, ROWS])
        con = sb("con", [P, CONSTS])
        ones = sb("ones", [P, P])
        zeros = sb("zeros", [P, P])
        xt = sb("xt", [P, D])
        zt = sb("zt", [P, D])
        xn = sb("xn", [P, D])
        xn2 = sb("xn2", [P, D])
        xT = sb("xT", [P, DB, P])
        kT2 = sb("kT2", [P, P])
        vmq = sb("vmq", [P, HD])
        stats = sb("stats", [P, 6])
        mv = sb("mv", [P, 2])
        rstd = sb("rstd", [P, 1])
        smax = sb("smax", [P, H])
        ssum = sb("ssum", [P, H])
        sinv = sb("sinv", [P, H])
        nrm = sb("nrm", [P, 2, H])
        rnrm = sb("rnrm", [P, 2, H])
        newt = sb("newt", [P, 2, H])
        rtab = sb("rtab", [P, 4, HD])
        zb = sb("zb", [P, D])
        oT_s = sb("oT_s", [P, 512])
        fcol = sb("fcol", [P, 2 * DB + 2 * FB])
        onat = sb("onat", [P, D])
        probsT = expd[:, 0, :].rearrange("p (h q) -> p h q", q=P)
        outT = expd[:, 1, 0:HP * P].rearrange("p (h q) -> p h q", q=P)
        gel = expd[:, 1, HP * P:HP * P + FB * P].rearrange("p (f q) -> p f q", q=P)
        wq_s, wk_s, wv_s, wxo_s = (wx[:, n] for n in range(4))
        ident = con[:, IDENT:IDENT + P]
        shiftm = con[:, SHIFT:SHIFT + P]

        def blocks(w):
            return w.rearrange("(b p) n -> p b n", p=P)

        ctx_v = blocks(ctxT)

        def bc(v, g, c):
            return v.unsqueeze(2).to_broadcast([P, g, c])

        def bg(v, g, c):
            return v.unsqueeze(1).to_broadcast([P, g, c])

        block = ctx.enter_context(nc.Block())

        @block.sync
        def _(sp):
            def load(dst, src, name):
                sp.dma_start(dst, src).then_inc(sem(name), 16)

            load(xt[:], x, "x_in")
            load(con[:], consts, "con_in")
            load(colv[:], cols, "col_in")
            load(wq_s, blocks(wqT), "wq_in")
            load(wk_s, blocks(wkT), "wk_in")

            for c in range(2):
                load(ctx1[:, c], ctx_v[:, :, c * C1:(c + 1) * C1], f"ctx1_in{c}")
            load(wv_s, blocks(wvT), "wv_in")
            load(rowv[:], rows.partition_broadcast(P), "row_in")
            load(wxo_s, blocks(woT), "wxo_in")
            load(aq_s[:], blocks(aq), "aq_in")
            load(akv_s[:], blocks(akv), "akv_in")
            load(ao_s[:], blocks(ao), "ao_in")
            for c in range(2):
                load(ctx2[:, c], ctx_v[:, :, c * C2:(c + 1) * C2], f"ctx2_in{c}")
            with sp.Fori(1, N1 // 2) as i:
                for b in range(2):
                    sp.wait_ge(sem("keys_projected"), i * 2 + (b - 1))
                    load(ctx1[:, b], ctx_v[:, :, bass.ds(i * (2 * C1) + b * C1, C1)], f"ctx1_in{b}")
            with sp.Fori(1, N2 // 2) as i:
                for b in range(2):
                    sp.wait_ge(sem("values_projected"), i * 2 + (b - 1))
                    load(ctx2[:, b], ctx_v[:, :, bass.ds(i * (2 * C2) + b * C2, C2)], f"ctx2_in{b}")

            def w2_loads(w2_i):
                load(w2_s[:, 0:FB - 1, :], w2_i[0:(FB - 1) * P, :].rearrange("(b p) n -> p b n", p=P), "w2_in")
                load(w2_s[0:FR, FB - 1, :], w2_i[(FB - 1) * P:FF, :], "w2_in")

            sp.wait_ge(sem("keys_staged"), N2)
            load(wqkv_s, blocks(wqkv[0]), "wqkv_in")
            load(wo_s, blocks(wo[0]), "wo_in")
            load(w1_s, blocks(w1[0]), "w1_in")
            w2_loads(w2[0])
            with sp.Fori(1, DEPTH) as i:
                sp.wait_ge(sem("v_projected"), i)
                load(wqkv_s, blocks(wqkv[bass.ds(i, 1)].rearrange("a c n -> (a c) n")), "wqkv_in")
                sp.wait_ge(sem("attn_projected"), i + 1)
                load(wo_s, blocks(wo[bass.ds(i, 1)].rearrange("a c n -> (a c) n")), "wo_in")
                sp.wait_ge(sem("lin_projected"), i)
                load(w1_s, blocks(w1[bass.ds(i, 1)].rearrange("a c n -> (a c) n")), "w1_in")
                sp.wait_ge(sem("ffn_projected"), i)
                w2_loads(w2[bass.ds(i, 1)].rearrange("a c n -> (a c) n"))
            sp.wait_ge(sem("result"), 1)
            load(out, xn[:], "stored")
            sp.wait_ge(sem("stored"), 16)

        @block.gpsimd
        def _(pool):
            nc.gpsimd.memset(ones[:], 1.0).then_inc(sem("ones_set"), 1)
            nc.gpsimd.memset(zeros[:], 0.0).then_inc(sem("zeros_set"), 1)
            nc.gpsimd.memset(vaug[:], 1.0).then_inc(sem("vaug_set"), 1)

            def stage_keys(c, b, free=None):
                if free is not None:
                    pool.wait_ge(sem("scores_ready"), free)
                nc.gpsimd.tensor_copy(keyst[:, b], keysT[:, :, bass.ds(c, C2)]).then_inc(sem("keys_staged"), 1)

            pool.wait_ge(sem("keys_kept"), N1)
            stage_keys(0, 0)
            stage_keys(C2, 1)
            with pool.Fori(1, N2 // 2) as i:
                for b in range(2):
                    stage_keys(i * (2 * C2) + b * C2, b, i * 4 + (2 * b - 2))

        @block.tensor
        def _(pe):
            mm = nc.tensor.matmul

            def project(dst, lhsT, rhs):
                for n, (a, b) in enumerate(zip(lhsT, rhs)):
                    last = mm(dst, a, b, start=n == 0, stop=n == len(lhsT) - 1)
                return last

            def transpose_blocks(dst, src, n=DB):
                for b in range(n):
                    last = nc.tensor.transpose(dst[:, b, :], src[:, b * P:(b + 1) * P], ident)
                return last

            pe.wait_ge(sem("con_in"), 16)
            pe.wait_ge(sem("xq_normed"), 1)
            transpose_blocks(banks(7, 1, P), xn).then_inc(sem("xq_turned"), 1)
            pe.wait_ge(sem("wq_in"), 16)
            pe.wait_ge(sem("xqT_ready"), 1)
            for t in range(DB):
                last = project(ps[:, 6, t * P:(t + 1) * P], [wq_s[:, b, t * P:(t + 1) * P] for b in range(DB)],
                               [xT[:, b, :] for b in range(DB)])
            last.then_inc(sem("queries_projected"), 1)

            def project_keys(c, b, arrived, free=None):
                pe.wait_ge(sem(f"ctx1_in{b}"), arrived)
                if free is not None:
                    pe.wait_ge(sem("keys_kept"), free)
                for t in range(DB):
                    last = project(ps[:, t, 0:C1], [wk_s[:, k, t * P:(t + 1) * P] for k in range(DB)],
                                   [ctx1[:, b, k, :] for k in range(DB)])
                last.then_inc(sem("keys_projected"), 1)

            def rough_scores(c, b, first=False):
                pe.wait_ge(sem("keys_kept"), c + 1)
                for hp in range(XH // 2):
                    if not (first and hp < 2):
                        pe.wait_ge(sem("maxima_taken"), c * 8 + (hp - 1))
                    for k in range(2):
                        t, j = divmod(2 * hp + k, HT)
                        last = mm(ps[:, 2 + 2 * (hp % 2) + k, 0:C1], qbd16[:, t, j, :], keys16[:, b, t, :],
                                  start=True, stop=True)
                    last.then_inc(sem("rough_ready"), 1)

            pe.wait_ge(sem("wk_in"), 16)
            project_keys(0, 0, 16)
            pe.wait_ge(sem("queries_rounded"), 1)
            project_keys(1, 1, 16, 1)
            rough_scores(0, 0, True)
            project_keys(2, 0, 32, 2)
            rough_scores(1, 1)
            with pe.Fori(1, N1 // 2 - 1) as i:
                project_keys(i * 2 + 1, 1, i * 16 + 16, i * 2 + 1)
                rough_scores(i * 2, 0)
                project_keys(i * 2 + 2, 0, i * 16 + 32, i * 2 + 2)
                rough_scores(i * 2 + 1, 1)
            project_keys(N1 - 1, 1, 8 * N1, N1 - 1)
            rough_scores(N1 - 2, 0)
            rough_scores(N1 - 1, 1)

            pe.wait_ge(sem("ones_set"), 1)
            pe.wait_ge(sem("maxima_spread"), 1)
            for n in range(4):
                last = mm(ps[:, n, :], ones[:], expd[:, 1, n * 512:(n + 1) * 512], start=True, stop=True)
            last.then_inc(sem("shift_summed"), 1)

            pe.wait_ge(sem("zeros_set"), 1)
            mm(ps[:, 4, :], zeros[:], qbd[:, 0, 0:4, :].rearrange("p a b -> p (a b)"), start=True, stop=False,
               skip_group_check=True)

            def scores(b, arrived, staged, taken=None, moved=None):
                pe.wait_ge(sem(f"ctx2_in{b}"), arrived)
                if moved is not None:
                    pe.wait_ge(sem("values_kept"), moved)
                project(ps[:, 5 + b, 0:D], [ctx2[:, b, k, :] for k in range(DB)],
                        [wv_s[:, k, :] for k in range(DB)]).then_inc(sem("values_projected"), 1)
                pe.wait_ge(sem("keys_staged"), staged)
                for t in range(DB):
                    if taken is not None:
                        pe.wait_ge(sem("scores_shifted"), taken + t)
                    for n in range(2):
                        last = mm(ps[:, 2 * t + n, :], keyst[:, b, t, :],
                                  qbd[:, t, 4 * n:4 * n + 4, :].rearrange("p a b -> p (a b)"), start=True, stop=True)
                    last.then_inc(sem("scores_ready"), 1)

            def weigh(c, b, last_step=False):
                pe.wait_ge(sem("values_kept"), c + 1)
                for t in range(DB):
                    pe.wait_ge(sem("exps_ready"), c * 2 + (t + 1))
                    for h in range(t * HT, (t + 1) * HT):
                        g, j = divmod(h, 4)
                        last = mm(ps[32 * j:32 * j + VW, 4, g * P:(g + 1) * P], vaug[:, b, h, :],
                                  expd[:, b, h * P:(h + 1) * P], start=False,
                                  stop=last_step, skip_group_check=True)
                last.then_inc(sem("step_weighed"), 1)

            pe.wait_ge(sem("wv_in"), 16)
            pe.wait_ge(sem("shift_ready"), 1)
            scores(0, 16, 1)
            scores(1, 16, 2, 1)
            weigh(0, 0)
            scores(0, 32, 3, 3, 1)
            weigh(1, 1)
            with pe.Fori(1, N2 // 2 - 1) as i:
                scores(1, i * 16 + 16, i * 2 + 2, i * 4 + 1, i * 2)
                weigh(i * 2, 0)
                scores(0, i * 16 + 32, i * 2 + 3, i * 4 + 3, i * 2 + 1)
                weigh(i * 2 + 1, 1)
            scores(1, 8 * N2, N2, 2 * N2 - 3, N2 - 2)
            weigh(N2 - 2, 0)
            weigh(N2 - 1, 1, True)

            pe.wait_ge(sem("xout_kept"), 1)
            transpose_blocks(banks(0, 1, P), oT_s, 4).then_inc(sem("xout_turned"), 1)
            pe.wait_ge(sem("xout_normed"), 1)
            transpose_blocks(banks(1, 1, P), onat).then_inc(sem("xnat_turned"), 1)
            pe.wait_ge(sem("xnatT_ready"), 1)
            pe.wait_ge(sem("wxo_in"), 16)
            project(ps[:, 2, 0:D], [xT[:, b, :] for b in range(DB)],
                    [wxo_s[:, b, :] for b in range(DB)]).then_inc(sem("xattn_projected"), 1)

            def attention(n, w, qT, kT, v):
                for s in range(H):
                    r, k = HD * (s // HP), s % HP
                    last = mm(banks(4, 4, P)[:, s, :], qT(k, r), kT(k, r), start=True, stop=True)
                last.then_inc(sem("sim_ready"), 1)
                pe.wait_ge(sem("probs_ready"), n)
                for s in range(H):
                    last = nc.tensor.transpose(banks(0, 4, P)[:, s, :], probs[:, s, :], ident)
                    if s == HP - 1:
                        last.then_inc(sem("probs_turned"), 1)
                last.then_inc(sem("probs_turned"), 1)
                for s in range(H):
                    if s == 0:
                        pe.wait_ge(sem("probsT_lo"), n)
                    if s == HP:
                        pe.wait_ge(sem("probsT_hi"), n)
                    r, k = HD * (s // HP), s % HP
                    last = mm(banks(4, 2, P)[r:r + HD, k, :], v(2 * k + s // HP), probsT[:, s, :],
                              start=True, stop=True)
                last.then_inc(sem("weighed"), 1)
                pe.wait_ge(sem("outT_ready"), n)
                project(ps[:, 6, 0:D], [outT[:, k, :] for k in range(HP)],
                        [w[:, k, :] for k in range(HP)]).then_inc(sem("attn_projected"), 1)

            pe.wait_ge(sem("xa_normed"), 1)
            transpose_blocks(banks(7, 1, P), xn2).then_inc(sem("xa_turned"), 1)
            pe.wait_ge(sem("xaT_ready"), 1)
            pe.wait_ge(sem("aq_in"), 16)
            pe.wait_ge(sem("akv_in"), 16)
            xTb = [xT[:, b, :] for b in range(DB)]
            for r in (0, HD):
                project(ps[r:r + HD, 2, 0:P], [akv_s[:, b, 0:HD] for b in range(DB)], xTb)
            project(ps[:, 3, 0:HD], xTb, [akv_s[:, b, HD:2 * HD] for b in range(DB)])\
                .then_inc(sem("mqa_kv_projected"), 1)
            for k in range(HP):
                last = project(banks(0, 2, P)[:, k, :], [aq_s[:, b, k * P:(k + 1) * P] for b in range(DB)], xTb)
            last.then_inc(sem("mqa_q_projected"), 1)
            pe.wait_ge(sem("mqa_kv_ready"), 1)
            pe.wait_ge(sem("mqa_q_ready"), 1)
            pe.wait_ge(sem("ao_in"), 16)
            attention(1, ao_s, lambda k, r: qkT[r:r + HD, k, :], lambda k, r: kT2[r:r + HD, :],
                      lambda h: vmq[:])

            with pe.Fori(0, DEPTH) as i:
                pe.wait_ge(sem("z_ready"), i * 2 + 1)
                mm(ps[:, 0, 0:P], zt[:, 0:P], ident, start=True, stop=True)
                mm(ps[:, 0, P:2 * P], zt[:, P:2 * P], shiftm, start=True, stop=True)\
                    .then_inc(sem("z_turned"), 1)
                pe.wait_ge(sem("zT_ready"), i + 1)
                pe.wait_ge(sem("wqkv_in"), i * 16 + 16)
                for n, name in enumerate(("q_projected", "k_projected", "v_projected")):
                    for k in range(2):
                        c0 = n * INNER + k * 512
                        last = project(ps[:, 2 + 2 * n + k, :], xTb, [wqkv_s[:, b, c0:c0 + 512] for b in range(DB)])
                    last.then_inc(sem(name), 1)
                for n, name in enumerate(("q", "k")):
                    pe.wait_ge(sem(f"{name}_rotated"), i + 1)
                    for k in range(HP):
                        src = rot[:, n * H + 2 * k:n * H + 2 * k + 2, :].rearrange("p a b -> p (a b)")
                        last = nc.tensor.transpose(banks(2 * n, 2, P)[:, k, :], src, ident)
                    last.then_inc(sem(f"{name}_turned"), 1)
                pe.wait_ge(sem("qT_ready"), i + 1)
                pe.wait_ge(sem("kT_ready"), i + 1)
                pe.wait_ge(sem("v_kept"), i + 1)
                pe.wait_ge(sem("wo_in"), i * 16 + 16)
                attention(i + 2, wo_s, lambda k, r: qkT[r:r + HD, k, :], lambda k, r: qkT[r:r + HD, HP + k, :],
                          lambda h: qkv_s[:, 2 * H + h, :])
                pe.wait_ge(sem("z_ready"), i * 2 + 2)
                mm(ps[:, 7, 0:P], shiftm, zt[:, P:2 * P], start=True, stop=True).then_inc(sem("z_shifted"), 1)
                pe.wait_ge(sem("f_normed"), i + 1)
                transpose_blocks(banks(0, 1, P), xn2).then_inc(sem("f_turned"), 1)
                pe.wait_ge(sem("fT_ready"), i + 1)
                pe.wait_ge(sem("w1_in"), i * 16 + 16)
                for g, b0, name in ((1, 3, "gate_projected"), (0, 1, "lin_projected")):
                    for f in range(FB):
                        m = P if f < FB - 1 else FR
                        c0 = g * FF + f * P
                        last = project(banks(b0, 2, P)[0:m, f, :], [w1_s[:, b, c0:c0 + m] for b in range(DB)], xTb)
                    last.then_inc(sem(name), 1)
                pe.wait_ge(sem("w2_in"), i * 32 + 32)
                pe.wait_ge(sem("u_ready"), i + 1)
                rowsof = [P] * (FB - 1) + [FR]
                project(ps[:, 5, 0:D], [uT[0:m, f, :] for f, m in enumerate(rowsof)],
                        [w2_s[0:m, f, :] for f, m in enumerate(rowsof)]).then_inc(sem("ffn_projected"), 1)

        @block.scalar
        def _(act):
            def copy(dst, src):
                return nc.scalar.activation(dst, src, ACT.Copy)

            act.wait_ge(sem("xq_turned"), 1)
            copy(xT[:], banks(7, 1, P)[:, 0:DB, :]).then_inc(sem("xqT_ready"), 1)

            act.wait_ge(sem("queries_ready"), 1)
            copy(qbd16[:], qbd[:]).then_inc(sem("queries_rounded"), 1)

            def keep_keys(c, b, free=None):
                act.wait_ge(sem("keys_projected"), c + 1)
                for t in range(DB):
                    nc.scalar.activation(keysT[:, t, bass.ds(c * C1, C1)], ps[:, t, 0:C1], ACT.Identity,
                                         bias=colv[:, BK + t:BK + t + 1])
                if free is not None:
                    act.wait_ge(sem("rough_ready"), free)
                for t in range(DB):
                    last = nc.scalar.activation(keys16[:, b, t, :], ps[:, t, 0:C1], ACT.Identity,
                                                bias=colv[:, BK + t:BK + t + 1])
                last.then_inc(sem("keys_kept"), 1)

            act.wait_ge(sem("col_in"), 16)
            keep_keys(0, 0)
            keep_keys(1, 1)
            with act.Fori(1, N1 // 2) as i:
                for b in range(2):
                    keep_keys(i * 2 + b, b, i * 16 + 8 * (b - 1))

            act.wait_ge(sem("shift_summed"), 1)
            copy(shift[:], ps[:, 0:4, :].rearrange("p a b -> p (a b)")).then_inc(sem("shift_ready"), 1)

            def exps(b, t, n):
                act.wait_ge(sem("scores_shifted"), n)
                half = expd[:, b, t * HT * P:(t + 1) * HT * P]
                nc.scalar.activation(half, half, ACT.Exp, scale=XS).then_inc(sem("exps_ready"), 1)

            with act.Fori(0, N2 // 2) as i:
                for b in range(2):
                    for t in range(DB):
                        exps(b, t, i * 4 + (2 * b + t + 1))

            act.wait_ge(sem("step_weighed"), N2)
            copy(oT_s[:], ps[:, 4, :]).then_inc(sem("xout_kept"), 1)
            act.wait_ge(sem("xnat_turned"), 1)
            copy(xT[:], banks(1, 1, P)[:, 0:DB, :]).then_inc(sem("xnatT_ready"), 1)

            def attention(n):
                act.wait_ge(sem("sim_shifted"), n)
                nc.scalar.activation(probs, probs, ACT.Exp).then_inc(sem("sim_exp"), 1)
                act.wait_ge(sem("probs_turned"), n * 2 - 1)
                copy(probsT[:, 0:HP, :], banks(0, 2, P)).then_inc(sem("probsT_lo"), 1)
                act.wait_ge(sem("weighed"), n)
                copy(outT, banks(4, 2, P)).then_inc(sem("outT_ready"), 1)

            act.wait_ge(sem("xa_turned"), 1)
            for b in range(DB):
                last = nc.scalar.activation(xT[:, b, :], ps[:, 7, b * P:(b + 1) * P], ACT.Identity,
                                            scale=colv[:, LNG + b:LNG + b + 1], bias=colv[:, LNB + b:LNB + b + 1])
            last.then_inc(sem("xaT_ready"), 1)
            act.wait_ge(sem("mqa_q_projected"), 1)
            copy(qkT[:, 0:HP, :], banks(0, 2, P)).then_inc(sem("mqa_q_ready"), 1)
            attention(1)

            with act.Fori(0, DEPTH) as i:
                act.wait_ge(sem("z_turned"), i + 1)
                copy(xT[:], banks(0, 1, P)[:, 0:DB, :]).then_inc(sem("zT_ready"), 1)
                for n, name in enumerate("qkv"):
                    act.wait_ge(sem(f"{name}_projected"), i + 1)
                    copy(qkv_s[:, n * H:(n + 1) * H, :], banks(2 + 2 * n, 2, HD)).then_inc(sem(f"{name}_kept"), 1)
                act.wait_ge(sem("q_turned"), i + 1)
                copy(qkT[:, 0:HP, :], banks(0, 2, P)).then_inc(sem("qT_ready"), 1)
                attention(i + 2)
                act.wait_ge(sem("f_turned"), i + 1)
                for b in range(DB):
                    last = nc.scalar.activation(xT[:, b, :], ps[:, 0, b * P:(b + 1) * P], ACT.Identity,
                                                scale=fcol[:, 2 * b:2 * b + 1], bias=fcol[:, 2 * b + 1:2 * b + 2])
                last.then_inc(sem("fT_ready"), 1)
                act.wait_ge(sem("gate_projected"), i + 1)
                for f in range(FB):
                    m = P if f < FB - 1 else FR
                    nc.scalar.activation(gel[0:m, f, :], banks(3, 2, P)[0:m, f, :], ACT.Gelu,
                                         bias=fcol[0:m, 2 * DB + FB + f:2 * DB + FB + f + 1])\
                        .then_inc(sem("gelu_ready"), 1)

        @block.vector
        def _(dve):
            V = nc.vector

            def link(ins, name, n=1):
                ins.then_inc(sem(name), 1)
                dve.wait_ge(sem(name), n)

            def inverse_root(y, v, a, name, n):
                steps = 1 + 3 * NEWTON
                link(V.tensor_scalar(y.bitcast(I32), v.bitcast(I32), -0.5, ROOT_GUESS, ALU.mult, ALU.add),
                     name + "_newton", n * steps + 1)
                for k in range(NEWTON):
                    link(V.tensor_tensor(a, y, y, ALU.mult), name + "_newton", n * steps + (3 * k + 2))
                    link(V.scalar_tensor_tensor(out=a, in0=a, scalar=-0.5, in1=v, op0=ALU.mult, op1=ALU.mult),
                         name + "_newton", n * steps + (3 * k + 3))
                    link(V.scalar_tensor_tensor(out=y, in0=a, scalar=1.5, in1=y, op0=ALU.add, op1=ALU.mult),
                         name + "_newton", n * steps + (3 * k + 4))

            def normalize(dst, src, name, n=0, between=None):
                link(V.bn_stats(stats[:], src), name + "_stats", n + 1)
                if between is not None:
                    between()
                link(V.bn_aggr(mv[:], stats[:]), name + "_moments", n + 1)
                link(V.tensor_scalar(mv[:, 1:2], mv[:, 1:2], EPS, None, ALU.add), name + "_eps", n + 1)
                inverse_root(rstd[:], mv[:, 1:2], newt[:, 0, 0:1], name, n)
                return V.tensor_scalar(dst, src, mv[:, 0:1], rstd[:, 0:1], ALU.subtract, ALU.mult)

            dve.wait_ge(sem("x_in"), 16)
            normalize(xn[:], xt[:], "xq").then_inc(sem("xq_normed"), 1)
            dve.wait_ge(sem("col_in"), 16)
            dve.wait_ge(sem("con_in"), 16)
            dve.wait_ge(sem("queries_projected"), 1)
            for t in range(DB):
                for j in range(HT):
                    last = V.tensor_scalar(qbd[:, t, j, :], ps[:, 6, t * P:(t + 1) * P], colv[:, BQ + t:BQ + t + 1],
                                           con[:, HEADM + j:HEADM + j + 1], ALU.add, ALU.mult)
            last.then_inc(sem("queries_ready"), 1)

            with dve.Fori(0, N1) as c:
                for hp in range(XH // 2):
                    dve.wait_ge(sem("rough_ready"), c * 8 + (hp + 1))
                    b0 = 2 + 2 * (hp % 2)
                    V.reduce_max(maxpart[:, bass.ds(c, 1), 2 * hp:2 * hp + 2].rearrange("p c h -> p (c h)"),
                                 ps[:, b0:b0 + 2, 0:C1], AX_X).then_inc(sem("maxima_taken"), 1)
            dve.wait_ge(sem("maxima_taken"), N1 * 8)
            link(V.reduce_max(xmax[:], maxpart[:].rearrange("p c h -> p h c"), AX_X), "xmax_ready")
            for h in range(XH):
                last = V.tensor_scalar(expd[:, 1, h * P:(h + 1) * P], ident, xmax[:, h:h + 1], None, ALU.mult)
            last.then_inc(sem("maxima_spread"), 1)
            dve.wait_ge(sem("vaug_set"), 1)
            dve.wait_ge(sem("shift_ready"), 1)

            def step(b, n, weighed=None):
                if weighed is not None:
                    dve.wait_ge(sem("step_weighed"), weighed)
                for t in range(DB):
                    dve.wait_ge(sem("scores_ready"), n + (t + 1))
                    cut = slice(t * HT * P, (t + 1) * HT * P)
                    V.tensor_tensor(expd[:, b, cut], ps[:, 2 * t:2 * t + 2, :].rearrange("p a b -> p (a b)"),
                                    shift[:, cut], ALU.subtract).then_inc(sem("scores_shifted"), 1)
                V.tensor_copy(vaug[:, b, :, 0:XD], ps[:, 5 + b, 0:D].rearrange("p (h d) -> p h d", d=XD))\
                    .then_inc(sem("values_kept"), 1)

            step(0, 0)
            step(1, 2)
            with dve.Fori(1, N2 // 2) as i:
                for b in range(2):
                    step(b, i * 4 + 2 * b, i * 2 + (b - 1))

            dve.wait_ge(sem("xout_turned"), 1)
            dve.wait_ge(sem("row_in"), 16)
            oview = ps[:, 0, :].rearrange("p (h c) -> p h c", c=32)
            link(V.reciprocal(sinv[:].unsqueeze(2), oview[:, :, XD:XD + 1]), "xsum_inverted")
            o3 = onat[:].rearrange("p (h d) -> p h d", d=XD)
            link(V.tensor_tensor(o3, oview[:, :, 0:XD], bc(sinv[:], XH, XD), ALU.mult), "xout_divided")
            V.tensor_tensor(onat[:], onat[:], rowv[:, BV:BV + D], ALU.add).then_inc(sem("xout_normed"), 1)
            link(V.tensor_tensor(zb[:], xt[:], rowv[:, BO:BO + D], ALU.add), "xb_ready")
            dve.wait_ge(sem("xattn_projected"), 1)
            link(V.tensor_tensor(xt[:], zb[:], ps[:, 2, 0:D], ALU.add), "x1_ready")

            def attention(n, scale, mask):
                dve.wait_ge(sem("sim_ready"), n)
                link(V.scalar_tensor_tensor(out=probs, in0=banks(4, 4, P), scalar=scale,
                                            in1=bg(con[:, mask:mask + P], H, P), op0=ALU.mult, op1=ALU.add),
                     "sim_masked", n)
                link(V.reduce_max(smax[:], probs, AX_X), "sim_max", n)
                V.tensor_tensor(probs, probs, bc(smax[:], H, P), ALU.subtract).then_inc(sem("sim_shifted"), 1)
                dve.wait_ge(sem("sim_exp"), n)
                link(V.reduce_sum(ssum[:], probs, AX_X), "sim_sum", n)
                link(V.reciprocal(sinv[:], ssum[:]), "sim_inverted", n)
                V.tensor_tensor(probs, probs, bc(sinv[:], H, P), ALU.mult).then_inc(sem("probs_ready"), 1)
                dve.wait_ge(sem("probs_turned"), n * 2)
                V.tensor_copy(probsT[:, HP:H, :], banks(2, 2, P)).then_inc(sem("probsT_hi"), 1)

            link(normalize(xn[:], xt[:], "x1"), "x1_normed")
            normalize(xn2[:], xn[:], "xa").then_inc(sem("xa_normed"), 1)
            dve.wait_ge(sem("mqa_kv_projected"), 1)
            V.tensor_copy(kT2[:], ps[:, 2, 0:P])
            V.tensor_copy(vmq[:], ps[:, 3, 0:HD]).then_inc(sem("mqa_kv_ready"), 1)
            attention(1, MQA_SCALE, CAUSAL)
            dve.wait_ge(sem("attn_projected"), 1)
            link(normalize(onat[:], ps[:, 6, 0:D], "ao"), "ao_normed")
            link(V.tensor_tensor(onat[:], onat[:], rowv[:, LOG:LOG + D], ALU.mult), "ao_scaled")
            link(V.tensor_tensor(zb[:], xt[:], rowv[:, LOB:LOB + D], ALU.add), "xlb_ready")
            link(V.tensor_tensor(xt[:], zb[:], onat[:], ALU.add), "x2_ready")
            normalize(zt[:], xt[:], "x2").then_inc(sem("z_ready"), 1)

            with dve.Fori(0, DEPTH) as i:
                V.tensor_copy(fcol[:, 0:2 * DB].rearrange("p (b g) -> p g b", g=2),
                              colv[:, FG:B1A].rearrange("p (g l b) -> p g l b", g=2, b=DB)[:, :, bass.ds(i, 1), :]
                              .rearrange("p g l b -> p g (l b)"))
                V.tensor_copy(fcol[:, 2 * DB:].rearrange("p (g f) -> p g f", g=2),
                              colv[:, B1A:COLS].rearrange("p (g l f) -> p g l f", g=2, f=FB)[:, :, bass.ds(i, 1), :]
                              .rearrange("p g l f -> p g (l f)")).then_inc(sem("fcol_ready"), 1)
                for n, (r0, c0, s0) in enumerate(((QSC, COSQ, SINQ), (KSC, COSK, SINK))):
                    sc = rowv[:, bass.ds(i * HD + r0, HD)]
                    V.tensor_tensor(rtab[:, 2 * n, :], con[:, c0:c0 + HD], sc, ALU.mult)
                    half = HD // 2
                    V.tensor_tensor(rtab[:, 2 * n + 1, 0:half], con[:, s0:s0 + half],
                                    rowv[:, bass.ds(i * HD + (r0 + half), half)], ALU.mult)
                    last = V.tensor_tensor(rtab[:, 2 * n + 1, half:HD], con[:, s0 + half:s0 + HD],
                                           rowv[:, bass.ds(i * HD + r0, half)], ALU.mult)
                link(last, "rotary_ready", i + 1)
                for n, name in enumerate("qk"):
                    src = qkv_s[:, n * H:(n + 1) * H, :]
                    dst = rot[:, n * H:(n + 1) * H, :]
                    half = HD // 2
                    dve.wait_ge(sem(f"{name}_kept"), i + 1)
                    V.tensor_tensor(dst, src, bg(rtab[:, 2 * n, :], H, HD), ALU.mult)
                    V.tensor_tensor(t2[:, :, 0:half], src[:, :, half:HD], bg(rtab[:, 2 * n + 1, 0:half], H, half),
                                    ALU.mult)
                    V.tensor_tensor(t2[:, :, half:HD], src[:, :, 0:half], bg(rtab[:, 2 * n + 1, half:HD], H, half),
                                    ALU.mult)
                    link(V.tensor_tensor(t1, src, src, ALU.mult), f"{name}_squared", i + 1)
                    link(V.reduce_sum(nrm[:, n, :], t1, AX_X), f"{name}_summed", i + 1)
                    link(V.tensor_scalar(nrm[:, n, :], nrm[:, n, :], NORM_FLOOR ** 2, None, ALU.max),
                         f"{name}_floored", i + 1)
                    inverse_root(rnrm[:, n, :], nrm[:, n, :], newt[:, n, :], name, i)
                    link(V.tensor_tensor(dst, dst, t2, ALU.add), f"{name}_turned_half", i + 1)
                    V.tensor_tensor(dst, dst, bc(rnrm[:, n, :], H, HD), ALU.mult).then_inc(sem(f"{name}_rotated"), 1)
                dve.wait_ge(sem("k_turned"), i + 1)
                V.tensor_copy(qkT[:, HP:, :], banks(2, 2, P)).then_inc(sem("kT_ready"), 1)
                attention(i + 2, QK_SCALE, BAND)
                dve.wait_ge(sem("attn_projected"), i + 2)
                V.tensor_tensor(zt[:], zt[:], ps[:, 6, 0:D], ALU.add).then_inc(sem("z_ready"), 1)
                dve.wait_ge(sem("z_ready"), i * 2 + 2)
                V.tensor_copy(xn[:, 0:P], zt[:, 0:P])
                dve.wait_ge(sem("z_shifted"), i + 1)
                link(V.tensor_copy(xn[:, P:D], ps[:, 7, 0:P]), "f_shifted", i + 1)

                def add_bias():
                    V.tensor_tensor(zb[:], zt[:], rowv[:, bass.ds(i * D + B2, D)], ALU.add).then_inc(sem("zb_ready"), 1)

                normalize(xn2[:], xn[:], "f", i, add_bias).then_inc(sem("f_normed"), 1)
                dve.wait_ge(sem("lin_projected"), i + 1)
                for f in range(FB):
                    m = P if f < FB - 1 else FR
                    dve.wait_ge(sem("gelu_ready"), i * FB + (f + 1))
                    last = V.scalar_tensor_tensor(out=uT[0:m, f, :], in0=banks(1, 2, P)[0:m, f, :],
                                                  scalar=fcol[0:m, 2 * DB + f:2 * DB + f + 1], in1=gel[0:m, f, :],
                                                  op0=ALU.add, op1=ALU.mult)
                last.then_inc(sem("u_ready"), 1)
                dve.wait_ge(sem("zb_ready"), i + 1)
                dve.wait_ge(sem("ffn_projected"), i + 1)
                V.tensor_tensor(zt[:], zb[:], ps[:, 5, 0:D], ALU.add).then_inc(sem("z_ready"), 1)
            dve.wait_ge(sem("z_ready"), 2 * DEPTH + 1)
            V.tensor_tensor(xn[:], xt[:], zt[:], ALU.add).then_inc(sem("result"), 1)


_OUT = (P, D)


def kernel(**inputs):
    import numpy as _np
    import concourse.bacc as _bacc
    from concourse import mybir as _mybir
    from concourse.bass_utils import run_bass_kernel_spmd as _run

    a = {k: _np.asarray(v) for k, v in inputs.items()}

    def turn(w):
        return _np.ascontiguousarray(w.T)

    def cols(v, n):
        v = v.reshape(-1, v.shape[-1])
        full = _np.zeros((v.shape[0], n * P), v.dtype)
        full[:, :v.shape[1]] = v
        return full.reshape(v.shape[0] * n, P).T

    b1 = a["L0_ffn_b1"]
    colv = _np.ascontiguousarray(_np.concatenate([
        cols(a["L0_xattn_b_q"], DB), cols(a["L0_xattn_b_k"], DB), cols(a["L0_attn_ln_g"], DB),
        cols(a["L0_attn_ln_b"], DB), cols(a["L0_ffn_ln_g"], DB), cols(a["L0_ffn_ln_b"], DB),
        cols(b1[:, :FF], FB), cols(b1[:, FF:], FB)], axis=1))
    rowv = _np.concatenate([a[k].reshape(-1) for k in (
        "L0_xattn_b_v", "L0_xattn_b_o", "L0_attn_lno_g", "L0_attn_lno_b", "L0_ffn_b2",
        "L0_ffn_q_scale", "L0_ffn_k_scale")])
    arrays = {
        "x_in_dram": _np.ascontiguousarray(a["x"][0]),
        "ctxT_dram": turn(a["ctx_1024"][0]),
        "wqT_dram": turn(a["L0_xattn_W_q"]), "wkT_dram": turn(a["L0_xattn_W_k"]),
        "wvT_dram": turn(a["L0_xattn_W_v"]), "woT_dram": turn(a["L0_xattn_W_o"]),
        "aq_dram": turn(a["L0_attn_w_q"]), "akv_dram": turn(a["L0_attn_w_kv"]), "ao_dram": turn(a["L0_attn_w_out"]),
        "wqkv_dram": _np.ascontiguousarray(a["L0_ffn_Wqkv"]), "wo_dram": _np.ascontiguousarray(a["L0_ffn_Wo"]),
        "w1_dram": _np.ascontiguousarray(a["L0_ffn_W1"]), "w2_dram": _np.ascontiguousarray(a["L0_ffn_W2"]),
        "cols_dram": colv, "rows_dram": rowv, "consts_dram": constants(),
    }
    nc = _bacc.Bacc("TRN2", target_bir_lowering=False, num_devices=1)
    args = [nc.dram_tensor(n, v.shape, _mybir.dt.from_np(v.dtype), kind="ExternalInput").ap()
            for n, v in arrays.items()]
    args.append(nc.dram_tensor("out_dram", _OUT, _mybir.dt.float32, kind="ExternalOutput").ap())
    build(nc, *args)
    r = _run(nc, [arrays], core_ids=[0])
    return r.results[0]["out_dram"].reshape(1, P, D)
```

```python
from contextlib import ExitStack

import concourse.bass as bass
import numpy as np
from concourse import mybir

F32 = mybir.dt.float32
BF16 = mybir.dt.bfloat16
I32 = mybir.dt.int32
ALU = mybir.AluOpType
ACT = mybir.ActivationFunctionType
AX_X = mybir.AxisListType.X

P = 128
D = 256
DB = D // P
S = 12544
XH, XD = 16, 16
HT = P // XD
XS = float(XD) ** -0.5
C1 = 448
N1 = S // C1
C2 = 128
N2 = S // C2
UNIT = 2 * C2
NU = S // UNIT
GR = 32
NG = D // GR
COPIED = (0, 1, 3, 4, 6, 7)
DIRECT = (2, 5)
VW = XD + 1
H, HD = 16, 64
INNER = H * HD
HP = H // 2
FF = 682
FB = -(-FF // P)
FR = FF - (FB - 1) * P
DEPTH = 6
WINDOW = 64
MQA_SCALE = float(HD) ** -1.0
QK_SCALE = 8.0
EPS = 1e-5
MASKED = -1e30
NORM_FLOOR = 1e-12
NEWTON = 3
ROOT_STEPS = 1 + 3 * NEWTON
ROOT_GUESS = float(0x5F3759DF)

IDENT, SHIFT, HEADM, GROUPM, CAUSAL, BAND, COSQ, SINQ, COSK, SINK, CONSTS = np.cumsum(
    [0, P, P, HT, 2, P, P, HD, HD, HD, HD]).tolist()
BQ, BK, LNG, LNB, FG, FBIAS, B1A, B1G, COLS = np.cumsum(
    [0, DB, DB, DB, DB, DB * DEPTH, DB * DEPTH, FB * DEPTH, FB * DEPTH]).tolist()
BV, BO, LOG, LOB, B2, QSC, KSC, ROWS = np.cumsum(
    [0, D, D, D, D, D * DEPTH, HD * DEPTH, HD * DEPTH]).tolist()


ROW_FEATURE = np.arange(D).reshape(DB, P // GR, GR).transpose(0, 2, 1).reshape(D)


def constants():
    t = np.zeros((P, CONSTS), np.float32)
    i = np.arange(P)
    t[:, IDENT:IDENT + P] = np.eye(P)
    t[:, SHIFT:SHIFT + P] = np.eye(P, k=1)
    feature = ROW_FEATURE[:P]
    t[:, HEADM:HEADM + HT] = feature[:, None] // XD == np.arange(HT)[None, :]
    t[:, GROUPM:GROUPM + 2] = feature[:, None] % GR // XD == np.arange(2)[None, :]
    q, k = i[:, None], i[None, :]
    t[:, CAUSAL:CAUSAL + P] = np.where(k > q, MASKED, 0.0)
    t[:, BAND:BAND + P] = np.where((k > q) | (q > k + WINDOW), MASKED, 0.0)
    half = np.arange(0, HD, 2, dtype=np.float32)
    freqs = i.astype(np.float32)[:, None] * (1.0 / 10000.0 ** (half / HD)).astype(np.float32)[None, :]
    base = (half + 0.4 * HD) / (1.4 * HD)
    power = (i - P // 2) / (WINDOW // 2)
    scale = (base[None, :].astype(np.float32) ** power[:, None].astype(np.float32)).astype(np.float32)
    cos, sin = np.cos(freqs), np.sin(freqs)
    for c0, s0, sc in ((COSQ, SINQ, scale), (COSK, SINK, 1.0 / scale)):
        t[:, c0:c0 + HD] = np.concatenate([cos * sc, cos * sc], 1)
        t[:, s0:s0 + HD] = np.concatenate([-sin * sc, sin * sc], 1)
    return t


def build(nc, x, ctxT, wqT, wkT, wvT, woT, aq, akv, ao, wqkv, wo, w1, w2, cols, rows, consts, out):
    with ExitStack() as ctx:
        def sb(name, shape, dt=F32):
            return ctx.enter_context(nc.sbuf_tensor(name, shape, dt))

        known = {}

        def sem(name):
            if name not in known:
                known[name] = ctx.enter_context(nc.semaphore(name))
            return known[name]

        ps = ctx.enter_context(nc.psum_tensor("ps", [P, 8, 512], F32))

        def banks(a, n, inner):
            return ps[:, a:a + n, :].rearrange("p b (g c) -> p (b g) c", c=inner)

        arena = sb("arena", [P, DB * S])
        keysT = arena[:].rearrange("p (t n) -> p t n", t=DB)
        place = [0]

        def view(n, c=None):
            v = arena[:, place[0]:place[0] + n]
            place[0] += n
            return v if c is None else v.rearrange("p (g c) -> p g c", c=c)

        wqkv_s = view(DB * 3 * INNER, 3 * INNER)
        wo_s = view(HP * D, D)
        w1_s = view(DB * 2 * FF, 2 * FF)
        w2_s = view(FB * D, D)
        qkv_s = view(3 * INNER, HD)
        rot = view(2 * INNER, HD)
        squares = view(2 * INNER, HD)
        aq_s = squares.rearrange("p g c -> p (g c)").rearrange("p (b n) -> p b n", b=DB)
        swapped = view(INNER, HD)
        qT_s = view(HP * P, P)
        kT_s = view(HP * 2 * P, 2 * P)
        assert place[0] <= DB * S

        qbd16 = sb("qbd16", [P, DB, HT, P], BF16)
        keys16 = sb("keys16", [P, 2, DB, C1], BF16)
        ctx1 = sb("ctx1", [P, 2, DB, C1])
        ctx2 = sb("ctx2", [P, 2, DB, UNIT])
        qstack = sb("qstack", [P, 2, NG, 2 * P], BF16)
        kstack = sb("kstack", [P, 2, NG, UNIT], BF16)
        queries = sb("queries", [P, DB, P])
        shift = sb("shift", [P, XH * P])
        expd = sb("expd", [P, 2, XH * P])
        vaug = sb("vaug", [P, 2, XH, VW])
        maxpart = sb("maxpart", [P, N1, XH])
        xmax = sb("xmax", [P, XH])
        wx = sb("wx", [P, 4, DB, D])
        akv_s = sb("akv_s", [P, DB, 2 * HD])
        ao_s = sb("ao_s", [P, HP, D])
        colv = sb("colv", [P, COLS])
        rowv = sb("rowv", [P, ROWS])
        con = sb("con", [P, CONSTS])
        ones16 = sb("ones16", [P, P], BF16)
        zeros = sb("zeros", [P, P])
        xt = sb("xt", [P, D])
        zt = sb("zt", [P, D])
        xn = sb("xn", [P, D])
        xn2 = sb("xn2", [P, D])
        xT = sb("xT", [P, DB, P])
        kT2 = sb("kT2", [P, 2 * P])
        masks16 = sb("masks16", [P, 2, 4, P], BF16)
        ident16 = sb("ident16", [P, P], BF16)
        warm = sb("warm", [P, 2])
        expbias = sb("expbias", [P, H])
        expscale = sb("expscale", [P, H])
        negscale = sb("negscale", [P, H])
        vmq = sb("vmq", [P, HD])
        stats = sb("stats", [P, 2, 6])
        mv = sb("mv", [P, 2])
        rstd = sb("rstd", [P, 1])
        smax = sb("smax", [P, H])
        ssum = sb("ssum", [P, H])
        sinv = sb("sinv", [P, H])
        nrm = sb("nrm", [P, 2, H])
        rnrm = sb("rnrm", [P, 2, H])
        newt = sb("newt", [P, 2, H])
        rtab = sb("rtab", [P, 4, HD])
        zb = sb("zb", [P, D])
        oT_s = ctx1[:].rearrange("p a b n -> p (a b n)")[:, 0:512]
        fcol = sb("fcol", [P, 2 * DB + 2 * FB])
        onat = queries[:].rearrange("p b q -> p (b q)")
        probs = shift[:].rearrange("p (h q) -> p h q", q=P)
        uT = ctx1[:].rearrange("p a b n -> p (a b n)")[:, 512:512 + FB * P].rearrange("p (f q) -> p f q", q=P)
        kparts = ctx1[:].rearrange("p a b n -> p (a b n)").bitcast(BF16)[:, 0:2 * 3 * DB * UNIT].rearrange(
            "p (u s b n) -> p u s b n", u=2, s=3, b=DB)
        krest = keys16[:].rearrange("p a b n -> p (a b n)").bitcast(F32)[:, 0:DB * UNIT].rearrange(
            "p (b n) -> p b n", b=DB)
        flatstack = kstack[:].rearrange("p u g n -> p (u g n)")
        qparts = flatstack[:, 0:3 * DB * P].rearrange("p (s b q) -> p s b q", s=3, b=DB)
        qdiag = flatstack[:, 3 * DB * P:3 * DB * P + 3 * DB * 2 * P].rearrange("p (s b n) -> p s b n", s=3, b=DB)
        rough = expd[:].rearrange("p a n -> p (a n)").bitcast(BF16)
        runmax = rough[:, 0:2 * len(COPIED) * C1].rearrange("p (a n) -> p a n", a=len(COPIED))
        spread = shift[:].bitcast(BF16)[:, 0:XH * P].rearrange("p (h q) -> p h q", q=P)
        copied = rough[:, 2 * len(COPIED) * C1:(2 * len(COPIED) + 4) * C1].rearrange("p (a n) -> p a n", a=2)
        probsT = expd[:, 0, :].rearrange("p (h q) -> p h q", q=P)
        outT = expd[:, 1, 0:HP * P].rearrange("p (h q) -> p h q", q=P)
        gel = expd[:, 1, HP * P:HP * P + FB * P].rearrange("p (f q) -> p f q", q=P)
        wq_s, wk_s, wv_s, wxo_s = (wx[:, n] for n in range(4))
        ident = con[:, IDENT:IDENT + P]
        shiftm = con[:, SHIFT:SHIFT + P]

        def blocks(w):
            return w.rearrange("(b p) n -> p b n", p=P)

        ctx_v = blocks(ctxT)

        def bc(v, g, c):
            return v.unsqueeze(2).to_broadcast([P, g, c])

        def bg(v, g, c):
            return v.unsqueeze(1).to_broadcast([P, g, c])

        def wait(eng, name, n):
            if not isinstance(n, int) or n > 0:
                eng.wait_ge(sem(name), n)

        def stacked(block, half_of, dst):
            rows_r = dst[GR * block:GR * (block + 1)]
            return [(rows_r[:, t * NG // DB:(t + 1) * NG // DB, :], half_of[:, t, :]) for t in range(DB)]

        block = ctx.enter_context(nc.Block())

        @block.sync
        def _(sp):
            def load(dst, src, name):
                sp.dma_start(dst, src).then_inc(sem(name), 16)

            load(xt[:], x, "x_in")
            load(con[:], consts, "con_in")
            load(colv[:], cols, "col_in")
            load(wq_s, blocks(wqT), "wq_in")
            load(wk_s, blocks(wkT), "wk_in")

            for c in range(2):
                load(ctx1[:, c], ctx_v[:, :, c * C1:(c + 1) * C1], f"ctx1_in{c}")
            load(wv_s, blocks(wvT), "wv_in")
            load(rowv[:], rows.partition_broadcast(P), "row_in")
            load(wxo_s, blocks(woT), "wxo_in")
            load(akv_s[:], blocks(akv), "akv_in")
            sp.wait_ge(sem("queries_split"), 1)
            sp.wait_ge(sem("qstack_zero"), 1)
            for half, parts in enumerate(((0, 0, 0, 1), (2, 1, 1))):
                for blk, s in enumerate(parts):
                    for dst, src in (stacked(blk, qdiag[:, s], qstack[:, half])):
                        load(dst, src, "queries_stacked")
            load(ao_s[:], blocks(ao), "ao_in")
            def load_values(u, b):
                wait(sp, "values_projected", u * 2 - 2)
                load(ctx2[:, b], ctx_v[:, :, bass.ds(u * UNIT, UNIT)], f"ctx2_in{b}")

            load_values(0, 0)
            load_values(1, 1)
            with sp.Fori(1, N1 // 2) as i:
                for b in range(2):
                    sp.wait_ge(sem("key_tiles_projected"), i * 4 + 2 * (b - 1))
                    load(ctx1[:, b], ctx_v[:, :, bass.ds(i * (2 * C1) + b * C1, C1)], f"ctx1_in{b}")

            def stack_keys(u, b):
                sp.wait_ge(sem("part3_ready"), u + 1)
                wait(sp, "scores_ready", u * 4 - 4)
                for blk, s in enumerate((0, 1, 2, 0)):
                    for dst, src in (stacked(blk, kparts[:, b, s], kstack[:, b])):
                        load(dst, src, f"stacked{b}")

            stack_keys(0, 0)
            stack_keys(1, 1)
            with sp.Fori(1, NU // 2) as i:
                for b in range(2):
                    load_values(i * 2 + b, b)
                    stack_keys(i * 2 + b, b)
            load_values(NU - 1, 0)
            stack_keys(NU - 1, 0)

            def w2_loads(w2_i):
                load(w2_s[:, 0:FB - 1, :], w2_i[0:(FB - 1) * P, :].rearrange("(b p) n -> p b n", p=P), "w2_in")
                load(w2_s[0:FR, FB - 1, :], w2_i[(FB - 1) * P:FF, :], "w2_in")

            sp.wait_ge(sem("rest_ready"), NU)
            load(aq_s, blocks(aq), "aq_in")
            load(wqkv_s, blocks(wqkv[0]), "wqkv_in")
            load(wo_s, blocks(wo[0]), "wo_in")
            load(w1_s, blocks(w1[0]), "w1_in")
            w2_loads(w2[0])
            with sp.Fori(1, DEPTH) as i:
                sp.wait_ge(sem("v_projected"), i * 2)
                load(wqkv_s, blocks(wqkv[bass.ds(i, 1)].rearrange("a c n -> (a c) n")), "wqkv_in")
                sp.wait_ge(sem("attn_projected"), i + 1)
                load(wo_s, blocks(wo[bass.ds(i, 1)].rearrange("a c n -> (a c) n")), "wo_in")
                sp.wait_ge(sem("lin_projected"), i)
                load(w1_s, blocks(w1[bass.ds(i, 1)].rearrange("a c n -> (a c) n")), "w1_in")
                sp.wait_ge(sem("ffn_projected"), i)
                w2_loads(w2[bass.ds(i, 1)].rearrange("a c n -> (a c) n"))
            sp.wait_ge(sem("result"), 1)
            load(out, xn[:], "stored")
            sp.wait_ge(sem("stored"), 16)

        @block.gpsimd
        def _(pool):
            nc.gpsimd.memset(runmax, -3e38).then_inc(sem("runmax_set"), 1)
            nc.gpsimd.memset(qstack[:, 1, :, :], 0.0).then_inc(sem("qstack_zero"), 1)
            nc.gpsimd.memset(ones16[:], 1.0).then_inc(sem("ones_set"), 1)
            nc.gpsimd.memset(zeros[:], 0.0).then_inc(sem("zeros_set"), 1)
            nc.gpsimd.memset(vaug[:], 1.0).then_inc(sem("vaug_set"), 1)

            nc.gpsimd.memset(kT2[:], 0.0).then_inc(sem("mqa_keys_zero"), 1)
            nc.gpsimd.memset(warm[:, 0:1], 0.0).then_inc(sem("gelu_warm"), 1)
            nc.gpsimd.memset(warm[:, 1:2], 0.0).then_inc(sem("exp_warm"), 1)
            pool.wait_ge(sem("con_in"), 16)
            nc.gpsimd.tensor_copy(ident16[:], ident)
            for m, c0 in enumerate((CAUSAL, BAND)):
                for k in range(4):
                    last = nc.gpsimd.tensor_copy(masks16[:, m, k, :], con[:, c0:c0 + P])
            last.then_inc(sem("masks_ready"), 1)

            def split_keys(u, b):
                pool.wait_ge(sem("part1_ready"), u + 1)
                wait(pool, "part3_ready", u)
                nc.gpsimd.tensor_tensor(krest, keysT[:, :, bass.ds(u * UNIT, UNIT)], kparts[:, b, 0], ALU.subtract)\
                    .then_inc(sem("rest_ready"), 1)
                pool.wait_ge(sem("part2_ready"), u + 1)
                nc.gpsimd.tensor_tensor(kparts[:, b, 2], krest, kparts[:, b, 1], ALU.subtract)\
                    .then_inc(sem("part3_ready"), 1)

            split_keys(0, 0)
            split_keys(1, 1)
            with pool.Fori(1, NU // 2) as i:
                for b in range(2):
                    split_keys(i * 2 + b, b)
            split_keys(NU - 1, 0)

            pool.wait_ge(sem("scores_ready"), 2 * N2)
            nc.gpsimd.memset(kT_s[:], 0.0).then_inc(sem("keys_zero"), 1)
            pool.wait_ge(sem("row_in"), 16)
            pool.wait_ge(sem("col_in"), 16)

            def layer_vectors(i):
                G = nc.gpsimd
                G.tensor_copy(fcol[:, 0:2 * DB].rearrange("p (b g) -> p g b", g=2),
                              colv[:, FG:B1A].rearrange("p (g l b) -> p g l b", g=2, b=DB)[:, :, bass.ds(i, 1), :]
                              .rearrange("p g l b -> p g (l b)"))
                G.tensor_copy(fcol[:, 2 * DB:].rearrange("p (g f) -> p g f", g=2),
                              colv[:, B1A:COLS].rearrange("p (g l f) -> p g l f", g=2, f=FB)[:, :, bass.ds(i, 1), :]
                              .rearrange("p g l f -> p g (l f)"))
                half = HD // 2
                for n, (r0, c0, s0) in enumerate(((QSC, COSQ, SINQ), (KSC, COSK, SINK))):
                    G.tensor_tensor(rtab[:, 2 * n, :], con[:, c0:c0 + HD], rowv[:, bass.ds(i * HD + r0, HD)], ALU.mult)
                    G.tensor_tensor(rtab[:, 2 * n + 1, 0:half], con[:, s0:s0 + half],
                                    rowv[:, bass.ds(i * HD + (r0 + half), half)], ALU.mult)
                    last = G.tensor_tensor(rtab[:, 2 * n + 1, half:HD], con[:, s0 + half:s0 + HD],
                                           rowv[:, bass.ds(i * HD + r0, half)], ALU.mult)
                last.then_inc(sem("layer_vectors_ready"), 1)

            layer_vectors(0)
            with pool.Fori(1, DEPTH) as i:
                pool.wait_ge(sem("u_ready"), i)
                layer_vectors(i)

        @block.tensor
        def _(pe):
            mm = nc.tensor.matmul

            def project(dst, lhsT, rhs):
                for n, (a, b) in enumerate(zip(lhsT, rhs)):
                    last = mm(dst, a, b, start=n == 0, stop=n == len(lhsT) - 1)
                return last

            def transpose_blocks(dst, src, n=DB):
                for b in range(n):
                    last = nc.tensor.transpose(dst[:, b, :], src[:, b * P:(b + 1) * P], ident)
                return last

            pe.wait_ge(sem("con_in"), 16)
            pe.wait_ge(sem("xq_normed"), 1)
            transpose_blocks(banks(7, 1, P), xn).then_inc(sem("xq_turned"), 1)
            pe.wait_ge(sem("wq_in"), 16)
            pe.wait_ge(sem("xqT_ready"), 1)
            for t in range(DB):
                last = project(ps[:, 6, t * P:(t + 1) * P], [wq_s[:, b, t * P:(t + 1) * P] for b in range(DB)],
                               [xT[:, b, :] for b in range(DB)])
            last.then_inc(sem("queries_projected"), 1)

            def project_piece(b, n):
                t, k = divmod(n, DB)
                last = mm(ps[:, t, 0:C1], wk_s[:, k, t * P:(t + 1) * P], ctx1[:, b, k, :],
                          start=k == 0, stop=k == DB - 1)
                if k == DB - 1:
                    last.then_inc(sem("key_tiles_projected"), 1)

            def rough_scores(c, b, arrived=None):
                pe.wait_ge(sem("keys_rounded"), c + 1)
                for hp in range(XH // 2):
                    if hp in COPIED:
                        a = COPIED.index(hp)
                        b0 = 4 + 2 * (a % 2)
                        wait(pe, "rough_copied", c * len(COPIED) + (a - 1))
                        done = "rough_for_copy"
                    else:
                        b0 = 2
                        wait(pe, "maxima_taken", c * len(DIRECT) + DIRECT.index(hp))
                        done = "rough_for_max"
                    for k in range(2):
                        t, j = divmod(2 * hp + k, HT)
                        last = mm(ps[:, b0 + k, 0:C1], qbd16[:, t, j, :], keys16[:, b, t, :], start=True, stop=True)
                    last.then_inc(sem(done), 1)
                    if arrived is not None and hp % 2 == 0:
                        if hp == 0:
                            pe.wait_ge(sem(f"ctx1_in{b}"), arrived)
                        if hp % 4 == 0:
                            pe.wait_ge(sem("key_tiles_kept"), c * 2 + (3 + hp // 4))
                        project_piece(b, hp // 2)

            pe.wait_ge(sem("wk_in"), 16)
            for b in range(2):
                pe.wait_ge(sem(f"ctx1_in{b}"), 16)
                for n in range(2 * DB):
                    if b and n % DB == 0:
                        pe.wait_ge(sem("key_tiles_kept"), n // DB + 1)
                    project_piece(b, n)
            pe.wait_ge(sem("queries_ready"), 1)
            rough_scores(0, 0, 32)
            rough_scores(1, 1, 32)
            with pe.Fori(1, N1 // 2 - 1) as i:
                rough_scores(i * 2, 0, i * 16 + 32)
                rough_scores(i * 2 + 1, 1, i * 16 + 32)
            rough_scores(N1 - 2, 0)
            rough_scores(N1 - 1, 1)

            pe.wait_ge(sem("ones_set"), 1)
            pe.wait_ge(sem("maxima_spread"), 1)
            for n in range(4):
                last = mm(ps[:, n, :], ones16[:], spread[:, 4 * n:4 * n + 4, :].rearrange("p a b -> p (a b)"),
                          start=True, stop=True)
            last.then_inc(sem("shift_summed"), 1)

            pe.wait_ge(sem("zeros_set"), 1)
            def scores(c, j, arrived):
                b, ub = j % 2, j // 2
                pe.wait_ge(sem(f"ctx2_in{ub}"), arrived * 16)
                wait(pe, "values_kept", c - 1)
                cs = slice(b * C2, (b + 1) * C2)
                project(ps[:, 5 + b, 0:D], [ctx2[:, ub, k, cs] for k in range(DB)],
                        [wv_s[:, k, :] for k in range(DB)]).then_inc(sem("values_projected"), 1)
                pe.wait_ge(sem(f"stacked{ub}"), arrived * (16 * 4 * DB))
                for t in range(DB):
                    wait(pe, "scores_shifted", c * 2 + (t - 1))
                    for g in range(4 * t, 4 * t + 4):
                        for part in range(2):
                            last = mm(ps[:, g // 2, (g % 2) * 2 * P:(g % 2 + 1) * 2 * P], kstack[:, ub, g, cs],
                                      qstack[:, part, g, :], start=part == 0, stop=part == 1)
                    last.then_inc(sem("scores_ready"), 1)

            def weigh(c, b, last_step=False):
                pe.wait_ge(sem("values_kept"), c + 1)
                for t in range(DB):
                    pe.wait_ge(sem("exps_ready"), c * 2 + (t + 1))
                    for h in range(t * HT, (t + 1) * HT):
                        g, j = divmod(h, 4)
                        last = mm(ps[32 * j:32 * j + VW, 4, g * P:(g + 1) * P], vaug[:, b, h, :],
                                  expd[:, b, h * P:(h + 1) * P], start=False,
                                  stop=last_step, skip_group_check=True)
                last.then_inc(sem("step_weighed"), 1)

            pe.wait_ge(sem("wv_in"), 16)
            pe.wait_ge(sem("shift_ready"), 1)
            mm(ps[:, 4, :], zeros[:], shift[:, 0:512], start=True, stop=False,
               skip_group_check=True)
            pe.wait_ge(sem("queries_stacked"), 16 * 7 * DB)
            for c in range(4):
                scores(c, c, 1)
                if c:
                    weigh(c - 1, (c - 1) % 2)
            with pe.Fori(1, N2 // 4) as i:
                for j in range(4):
                    scores(i * 4 + j, j, i + 1)
                    weigh(i * 4 + (j - 1), (j - 1) % 2)
            for c in (N2 - 2, N2 - 1):
                scores(c, c % 4, N2 // 4 + 1)
                weigh(c - 1, (c - 1) % 2)
            weigh(N2 - 1, 1, True)

            pe.wait_ge(sem("xout_kept"), 1)
            transpose_blocks(banks(0, 1, P), oT_s, 4).then_inc(sem("xout_turned"), 1)
            pe.wait_ge(sem("xout_normed"), 1)
            transpose_blocks(banks(1, 1, P), onat).then_inc(sem("xnat_turned"), 1)
            pe.wait_ge(sem("xnatT_ready"), 1)
            pe.wait_ge(sem("wxo_in"), 16)
            project(ps[:, 2, 0:D], [xT[:, b, :] for b in range(DB)],
                    [wxo_s[:, b, :] for b in range(DB)]).then_inc(sem("xattn_projected"), 1)

            def attention(n4, n, w, mask, qT, kT, v):
                for b in range(4):
                    mm(ps[:, 4 + b, :], ident16[:], masks16[:, mask].rearrange("p a b -> p (a b)"),
                       start=True, stop=False)
                    for k in (2 * b, 2 * b + 1):
                        last = mm(banks(4, 4, 2 * P)[:, k, :], qT(k), kT(k), start=False, stop=k % 2 == 1)
                    last.then_inc(sem("sim_ready"), 1)
                for b in range(4):
                    pe.wait_ge(sem("probs_ready"), n4 + (b + 1))
                    for h in range(4 * b, 4 * b + 4):
                        last = nc.tensor.transpose(banks(0, 4, P)[:, h, :], probs[:, h, :], ident)
                    last.then_inc(sem("probs_turned"), 1)
                for b in range(4):
                    if b % 2 == 0:
                        pe.wait_ge(sem("probsT_even"), n * 2 + (b // 2 - 1))
                    else:
                        pe.wait_ge(sem("probsT_odd"), n * 2 + (b // 2 - 1))
                    for h in range(4 * b, 4 * b + 4):
                        r = HD * (h % 2)
                        last = mm(banks(4, 2, P)[r:r + HD, h // 2, :], v(h), probsT[:, h, :], start=True, stop=True)
                    if b % 2:
                        last.then_inc(sem("weighed"), 1)
                pe.wait_ge(sem("outT_lo"), n)
                for k in range(HP):
                    if k == HP // 2:
                        pe.wait_ge(sem("outT_hi"), n)
                    last = mm(ps[:, 6, 0:D], outT[:, k, :], w[:, k, :], start=k == 0, stop=k == HP - 1)
                last.then_inc(sem("attn_projected"), 1)

            pe.wait_ge(sem("xa_normed"), 1)
            transpose_blocks(banks(7, 1, P), xn2).then_inc(sem("xa_turned"), 1)
            pe.wait_ge(sem("xaT_ready"), 1)
            pe.wait_ge(sem("aq_in"), 16)
            pe.wait_ge(sem("akv_in"), 16)
            xTb = [xT[:, b, :] for b in range(DB)]
            for r in (0, HD):
                project(ps[r:r + HD, 2, 0:P], [akv_s[:, b, 0:HD] for b in range(DB)], xTb)
            project(ps[:, 3, 0:HD], xTb, [akv_s[:, b, HD:2 * HD] for b in range(DB)])\
                .then_inc(sem("mqa_kv_projected"), 1)
            for k in range(HP):
                last = project(banks(0, 2, P)[:, k, :], [aq_s[:, b, k * P:(k + 1) * P] for b in range(DB)], xTb)
            last.then_inc(sem("mqa_q_projected"), 1)
            pe.wait_ge(sem("mqa_kv_ready"), 1)
            pe.wait_ge(sem("mqa_q_ready"), 1)
            pe.wait_ge(sem("ao_in"), 16)
            pe.wait_ge(sem("masks_ready"), 1)
            attention(0, 1, ao_s, 0, lambda k: qT_s[:, k, :], lambda k: kT2[:], lambda h: vmq[:])

            with pe.Fori(0, DEPTH) as i:
                pe.wait_ge(sem("z_ready"), i * 2 + 1)
                mm(ps[:, 0, 0:P], zt[:, 0:P], ident, start=True, stop=True)
                mm(ps[:, 0, P:2 * P], zt[:, P:2 * P], shiftm, start=True, stop=True)\
                    .then_inc(sem("z_turned"), 1)
                pe.wait_ge(sem("zT_ready"), i + 1)
                pe.wait_ge(sem("wqkv_in"), i * 16 + 16)
                for name, n in (("k", 1), ("q", 0), ("v", 2)):
                    for k in range(2):
                        c0 = n * INNER + k * 512
                        project(ps[:, 2 + 2 * n + k, :], xTb, [wqkv_s[:, b, c0:c0 + 512] for b in range(DB)])\
                            .then_inc(sem(f"{name}_projected"), 1)
                for name, n, b0 in (("k", 1, 0), ("q", 0, 2)):
                    pe.wait_ge(sem(f"{name}_rotated"), i + 1)
                    for k in range(HP):
                        src = rot[:, n * H + 2 * k:n * H + 2 * k + 2, :].rearrange("p a b -> p (a b)")
                        last = nc.tensor.transpose(banks(b0, 2, P)[:, k, :], src, ident)
                    last.then_inc(sem(f"{name}_turned"), 1)
                pe.wait_ge(sem("qT_ready"), i + 1)
                pe.wait_ge(sem("kT_lo"), i + 1)
                pe.wait_ge(sem("kT_hi"), i + 1)
                pe.wait_ge(sem("v_half_kept"), i * 2 + 2)
                pe.wait_ge(sem("wo_in"), i * 16 + 16)
                attention(i * 4 + 4, i + 2, wo_s, 1, lambda k: qT_s[:, k, :], lambda k: kT_s[:, k, :],
                          lambda h: qkv_s[:, 2 * H + h, :])
                pe.wait_ge(sem("z_ready"), i * 2 + 2)
                mm(ps[:, 7, 0:P], shiftm, zt[:, P:2 * P], start=True, stop=True).then_inc(sem("z_shifted"), 1)
                pe.wait_ge(sem("f_normed"), i + 1)
                transpose_blocks(banks(0, 1, P), xn2).then_inc(sem("f_turned"), 1)
                pe.wait_ge(sem("fT_ready"), i + 1)
                pe.wait_ge(sem("w1_in"), i * 16 + 16)
                for g, b0, name in ((1, 3, "gate_projected"), (0, 1, "lin_projected")):
                    for f in range(FB):
                        m = P if f < FB - 1 else FR
                        c0 = g * FF + f * P
                        last = project(banks(b0, 2, P)[0:m, f, :], [w1_s[:, b, c0:c0 + m] for b in range(DB)], xTb)
                    last.then_inc(sem(name), 1)
                pe.wait_ge(sem("w2_in"), i * 32 + 32)
                pe.wait_ge(sem("u_ready"), i + 1)
                rowsof = [P] * (FB - 1) + [FR]
                project(ps[:, 5, 0:D], [uT[0:m, f, :] for f, m in enumerate(rowsof)],
                        [w2_s[0:m, f, :] for f, m in enumerate(rowsof)]).then_inc(sem("ffn_projected"), 1)

        @block.scalar
        def _(act):
            def copy(dst, src):
                return nc.scalar.activation(dst, src, ACT.Copy)

            act.wait_ge(sem("xq_turned"), 1)
            copy(xT[:], banks(7, 1, P)[:, 0:DB, :]).then_inc(sem("xqT_ready"), 1)

            def keep_tile(c, t):
                act.wait_ge(sem("key_tiles_projected"), c * 2 + (t + 1))
                nc.scalar.activation(keysT[:, t, bass.ds(c * C1, C1)], ps[:, t, 0:C1], ACT.Identity,
                                     bias=colv[:, BK + t:BK + t + 1]).then_inc(sem("key_tiles_kept"), 1)

            def copy_rough(c, next_two=True, next_one=True):
                for a in range(len(COPIED)):
                    n = c * len(COPIED) + a
                    act.wait_ge(sem("rough_for_copy"), n + 1)
                    wait(act, "maxima_merged", n - 1)
                    copy(copied[:, a % 2].rearrange("p (k n) -> p k n", k=2),
                         ps[:, 4 + 2 * (a % 2):6 + 2 * (a % 2), 0:C1]).then_inc(sem("rough_copied"), 1)
                    if a == 0 and next_one:
                        keep_tile(c + 1, 1)
                    if a == 3 and next_two:
                        keep_tile(c + 2, 0)

            act.wait_ge(sem("col_in"), 16)
            keep_tile(0, 0)
            keep_tile(0, 1)
            keep_tile(1, 0)
            copy_rough(0)
            copy_rough(1)
            with act.Fori(1, N1 // 2 - 1) as i:
                for b in range(2):
                    copy_rough(i * 2 + b)
            copy_rough(N1 - 2, False)
            copy_rough(N1 - 1, False, False)

            def first_part(u, b):
                wait(act, f"stacked{b}", (u - b) * (8 * 4 * DB))
                copy(kparts[:, b, 0], keysT[:, :, bass.ds(u * UNIT, UNIT)]).then_inc(sem("part1_ready"), 1)

            def second_part(u, b):
                act.wait_ge(sem("rest_ready"), u + 1)
                copy(kparts[:, b, 1], krest).then_inc(sem("part2_ready"), 1)

            for u in range(2):
                first_part(u, u)
                second_part(u, u)
            act.wait_ge(sem("shift_summed"), 1)
            copy(shift[:], ps[:, 0:4, :].rearrange("p a b -> p (a b)")).then_inc(sem("shift_ready"), 1)

            def exps(c, b, t):
                act.wait_ge(sem("scores_shifted"), c * 2 + (t + 1))
                half = expd[:, b, t * HT * P:(t + 1) * HT * P]
                nc.scalar.activation(half, half, ACT.Exp, scale=XS).then_inc(sem("exps_ready"), 1)

            def unit(u, b, ahead=True):
                exps(u * 2, 0, 0)
                if ahead:
                    first_part(u + 2, b)
                exps(u * 2, 0, 1)
                exps(u * 2 + 1, 1, 0)
                if ahead:
                    second_part(u + 2, b)
                exps(u * 2 + 1, 1, 1)

            with act.Fori(0, NU // 2 - 1) as i:
                for b in range(2):
                    unit(i * 2 + b, b)
            unit(NU - 3, 0)
            unit(NU - 2, 1, False)
            unit(NU - 1, 0, False)

            act.wait_ge(sem("step_weighed"), N2)
            copy(oT_s, ps[:, 4, :]).then_inc(sem("xout_kept"), 1)
            act.wait_ge(sem("xnat_turned"), 1)
            copy(xT[:], banks(1, 1, P)[:, 0:DB, :]).then_inc(sem("xnatT_ready"), 1)

            def attention(n4, n):
                for h in range(H):
                    if h % 4 == 0:
                        act.wait_ge(sem("bias_ready"), n4 + (h // 4 + 1))
                    last = nc.scalar.activation(probs[:, h, :], banks(4, 4, P)[:, h, :], ACT.Exp,
                                                scale=expscale[:, h:h + 1], bias=expbias[:, h:h + 1],
                                                accum_out=ssum[:, h:h + 1])
                    if h % 4 == 3:
                        last.then_inc(sem("sim_exp"), 1)

            def turned(n4, n):
                for b in (0, 2):
                    act.wait_ge(sem("probs_turned"), n4 + (b + 1))
                    copy(probsT[:, 4 * b:4 * b + 4, :], banks(b, 1, P)).then_inc(sem("probsT_even"), 1)
                act.wait_ge(sem("weighed"), n * 2 - 1)
                copy(outT[:, 0:4, :], banks(4, 1, P)).then_inc(sem("outT_lo"), 1)

            act.wait_ge(sem("xa_turned"), 1)
            for b in range(DB):
                last = nc.scalar.activation(xT[:, b, :], ps[:, 7, b * P:(b + 1) * P], ACT.Identity,
                                            scale=colv[:, LNG + b:LNG + b + 1], bias=colv[:, LNB + b:LNB + b + 1])
            last.then_inc(sem("xaT_ready"), 1)
            act.wait_ge(sem("mqa_q_projected"), 1)
            copy(qT_s, banks(0, 2, P)).then_inc(sem("mqa_q_ready"), 1)
            attention(0, 1)
            turned(0, 1)

            with act.Fori(0, DEPTH) as i:
                act.wait_ge(sem("z_turned"), i + 1)
                copy(xT[:], banks(0, 1, P)[:, 0:DB, :]).then_inc(sem("zT_ready"), 1)
                for name, n in (("k", 1), ("q", 0), ("v", 2)):
                    for k in range(2):
                        act.wait_ge(sem(f"{name}_projected"), i * 2 + (k + 1))
                        h0 = n * H + k * HP
                        copy(qkv_s[:, h0:h0 + HP, :], banks(2 + 2 * n + k, 1, HD)).then_inc(sem(f"{name}_half_kept"), 1)
                    if name == "v":
                        break
                    act.wait_ge(sem(f"{name}_half_kept"), i * 2 + 2)
                    nc.scalar.activation(squares[:, n * H:(n + 1) * H, :], qkv_s[:, n * H:(n + 1) * H, :], ACT.Square)\
                        .then_inc(sem(f"{name}_squared"), 1)
                act.wait_ge(sem("k_turned"), i + 1)
                copy(kT_s[0:HD, :, 0:P], banks(0, 2, P)[0:HD]).then_inc(sem("kT_lo"), 1)
                act.wait_ge(sem("q_turned"), i + 1)
                copy(qT_s, banks(2, 2, P)).then_inc(sem("qT_ready"), 1)
                attention(i * 4 + 4, i + 2)
                act.wait_ge(sem("gelu_warm"), i + 1)
                nc.scalar.activation(warm[:, 0:1], con[:, IDENT:IDENT + 1], ACT.Gelu).then_inc(sem("gelu_warm"), 1)
                turned(i * 4 + 4, i + 2)
                act.wait_ge(sem("f_turned"), i + 1)
                for b in range(DB):
                    last = nc.scalar.activation(xT[:, b, :], ps[:, 0, b * P:(b + 1) * P], ACT.Identity,
                                                scale=fcol[:, 2 * b:2 * b + 1], bias=fcol[:, 2 * b + 1:2 * b + 2])
                last.then_inc(sem("fT_ready"), 1)
                act.wait_ge(sem("gate_projected"), i + 1)
                for f in range(FB):
                    m = P if f < FB - 1 else FR
                    nc.scalar.activation(gel[0:m, f, :], banks(3, 2, P)[0:m, f, :], ACT.Gelu,
                                         bias=fcol[0:m, 2 * DB + FB + f:2 * DB + FB + f + 1])\
                        .then_inc(sem("gelu_ready"), 1)
                act.wait_ge(sem("exp_warm"), i + 1)
                nc.scalar.activation(warm[:, 1:2], con[:, IDENT:IDENT + 1], ACT.Exp).then_inc(sem("exp_warm"), 1)

        @block.vector
        def _(dve):
            V = nc.vector

            def link(ins, name, n=1):
                ins.then_inc(sem(name), 1)
                dve.wait_ge(sem(name), n)

            def inverse_root(y, v, a, name, n):
                link(V.tensor_scalar(y.bitcast(I32), v.bitcast(I32), -0.5, ROOT_GUESS, ALU.mult, ALU.add),
                     name, n + 1)
                for k in range(NEWTON):
                    link(V.tensor_tensor(a, y, y, ALU.mult), name, n + (3 * k + 2))
                    link(V.scalar_tensor_tensor(out=a, in0=a, scalar=-0.5, in1=v, op0=ALU.mult, op1=ALU.mult),
                         name, n + (3 * k + 3))
                    link(V.scalar_tensor_tensor(out=y, in0=a, scalar=1.5, in1=y, op0=ALU.add, op1=ALU.mult),
                         name, n + (3 * k + 4))

            def normalize(dst, src, run):
                n = run * (3 + ROOT_STEPS)
                link(V.bn_stats(stats[:, 0, :], src), "norm_steps", n + 1)
                link(V.bn_aggr(mv[:], stats[:, 0, :]), "norm_steps", n + 2)
                link(V.tensor_scalar(mv[:, 1:2], mv[:, 1:2], EPS, None, ALU.add), "norm_steps", n + 3)
                inverse_root(rstd[:], mv[:, 1:2], newt[:, 0, 0:1], "norm_steps", n + 3)
                return V.tensor_scalar(dst, src, mv[:, 0:1], rstd[:, 0:1], ALU.subtract, ALU.mult)

            V.memset(expscale[:], MQA_SCALE)
            V.memset(negscale[:], -MQA_SCALE)
            dve.wait_ge(sem("x_in"), 16)
            normalize(xn[:], xt[:], 0).then_inc(sem("xq_normed"), 1)
            dve.wait_ge(sem("col_in"), 16)
            dve.wait_ge(sem("con_in"), 16)
            dve.wait_ge(sem("queries_projected"), 1)
            for t in range(DB):
                for j in range(HT):
                    V.tensor_scalar(qbd16[:, t, j, :], ps[:, 6, t * P:(t + 1) * P], colv[:, BQ + t:BQ + t + 1],
                                    con[:, HEADM + j:HEADM + j + 1], ALU.add, ALU.mult)
                last = V.tensor_scalar(queries[:, t, :], ps[:, 6, t * P:(t + 1) * P], colv[:, BQ + t:BQ + t + 1],
                                       None, ALU.add)
            last.then_inc(sem("queries_ready"), 1)

            def round_keys(c, b):
                dve.wait_ge(sem("key_tiles_kept"), c * 2 + 2)
                wait(dve, "rough_for_copy", (c - 1) * len(COPIED))
                wait(dve, "rough_for_max", (c - 1) * len(DIRECT))
                V.tensor_copy(keys16[:, b], keysT[:, :, bass.ds(c * C1, C1)]).then_inc(sem("keys_rounded"), 1)

            def take_maxima(c, b, more=True):
                for hp in range(XH // 2):
                    if hp in COPIED:
                        a = COPIED.index(hp)
                        n = c * len(COPIED) + a
                        dve.wait_ge(sem("rough_copied"), n + 1)
                        V.tensor_tensor(runmax[:, a], runmax[:, a], copied[:, a % 2], ALU.max)\
                            .then_inc(sem("maxima_merged"), 1)
                    else:
                        dve.wait_ge(sem("rough_for_max"), c * len(DIRECT) + (DIRECT.index(hp) + 1))
                        V.reduce_max(maxpart[:, bass.ds(c, 1), 2 * hp:2 * hp + 2].rearrange("p c h -> p (c h)"),
                                     ps[:, 2:4, 0:C1], AX_X).then_inc(sem("maxima_taken"), 1)
                    if hp == 3 and more:
                        round_keys(c + 1, 1 - b)

            round_keys(0, 0)
            dve.wait_ge(sem("queries_ready"), 1)
            left = queries
            for part in range(3):
                link(V.tensor_copy(qparts[:, part], left[:]), "query_part", 2 * part + 1)
                for k in range(2):
                    last = V.tensor_scalar(qdiag[:, part, :, k * P:(k + 1) * P], qparts[:, part],
                                           con[:, GROUPM + k:GROUPM + k + 1], None, ALU.mult)
                if part < 2:
                    link(V.tensor_tensor(queries[:], queries[:], qparts[:, part], ALU.subtract),
                         "query_part", 2 * part + 2)
            last.then_inc(sem("queries_split"), 1)
            dve.wait_ge(sem("runmax_set"), 1)
            take_maxima(0, 0)
            take_maxima(1, 1)
            with dve.Fori(1, N1 // 2 - 1) as i:
                for b in range(2):
                    take_maxima(i * 2 + b, b)
            take_maxima(N1 - 2, 0)
            take_maxima(N1 - 1, 1, False)
            dve.wait_ge(sem("masks_ready"), 1)
            dve.wait_ge(sem("maxima_merged"), N1 * len(COPIED))
            rm = runmax.rearrange("p a (k n) -> p (a k) n", k=2)
            for fold in range(2):
                n = C1 >> (fold + 1)
                link(V.tensor_tensor(rm[:, :, 0:n], rm[:, :, 0:n], rm[:, :, n:2 * n], ALU.max), "folded", fold + 1)
            for a, hp in enumerate(COPIED):
                V.reduce_max(xmax[:, 2 * hp:2 * hp + 2], rm[:, 2 * a:2 * a + 2, 0:C1 // 4], AX_X)
            dve.wait_ge(sem("maxima_taken"), N1 * len(DIRECT))
            for hp in DIRECT:
                last = V.reduce_max(xmax[:, 2 * hp:2 * hp + 2],
                                    maxpart[:, :, 2 * hp:2 * hp + 2].rearrange("p c h -> p h c"), AX_X)
            link(last, "xmax_ready")
            for h in range(XH):
                last = V.tensor_scalar(spread[:, h, :], ident16[:], xmax[:, h:h + 1], None, ALU.mult)
            last.then_inc(sem("maxima_spread"), 1)
            dve.wait_ge(sem("vaug_set"), 1)
            dve.wait_ge(sem("shift_ready"), 1)

            def step(b, n, weighed=None):
                if weighed is not None:
                    dve.wait_ge(sem("step_weighed"), weighed)
                for t in range(DB):
                    dve.wait_ge(sem("scores_ready"), n + (t + 1))
                    cut = slice(t * HT * P, (t + 1) * HT * P)
                    V.tensor_tensor(expd[:, b, cut], ps[:, 2 * t:2 * t + 2, :].rearrange("p a b -> p (a b)"),
                                    shift[:, cut], ALU.subtract).then_inc(sem("scores_shifted"), 1)
                V.tensor_copy(vaug[:, b, :, 0:XD], ps[:, 5 + b, 0:D].rearrange("p (h d) -> p h d", d=XD))\
                    .then_inc(sem("values_kept"), 1)

            step(0, 0)
            step(1, 2)
            with dve.Fori(1, N2 // 2) as i:
                for b in range(2):
                    step(b, i * 4 + 2 * b, i * 2 + (b - 1))

            dve.wait_ge(sem("xout_turned"), 1)
            dve.wait_ge(sem("row_in"), 16)
            oview = ps[:, 0, :].rearrange("p (h c) -> p h c", c=32)
            link(V.reciprocal(sinv[:].unsqueeze(2), oview[:, :, XD:XD + 1]), "xsum_inverted")
            o3 = onat.rearrange("p (h d) -> p h d", d=XD)
            link(V.tensor_tensor(o3, oview[:, :, 0:XD], bc(sinv[:], XH, XD), ALU.mult), "xout_divided")
            V.tensor_tensor(onat, onat, rowv[:, BV:BV + D], ALU.add).then_inc(sem("xout_normed"), 1)
            link(V.tensor_tensor(zb[:], xt[:], rowv[:, BO:BO + D], ALU.add), "xb_ready")
            dve.wait_ge(sem("xattn_projected"), 1)
            link(V.tensor_tensor(xt[:], zb[:], ps[:, 2, 0:D], ALU.add), "x1_ready")

            def attention(n4, n, negscale):
                for b in range(4):
                    dve.wait_ge(sem("sim_ready"), n4 + (b + 1))
                    hs = slice(4 * b, 4 * b + 4)
                    link(V.reduce_max(smax[:, hs], banks(4 + b, 1, P), AX_X), "sim_max", n4 + (b + 1))
                    V.tensor_tensor(expbias[:, hs], smax[:, hs], negscale[:, hs], ALU.mult)\
                        .then_inc(sem("bias_ready"), 1)
                for b in range(4):
                    hs = slice(4 * b, 4 * b + 4)
                    dve.wait_ge(sem("sim_exp"), n4 + (b + 1))
                    link(V.reciprocal(sinv[:, hs], ssum[:, hs]), "sim_inverted", n4 + (b + 1))
                    V.tensor_tensor(probs[:, hs, :], probs[:, hs, :], bc(sinv[:, hs], 4, P), ALU.mult)\
                        .then_inc(sem("probs_ready"), 1)
                for b in (1, 3):
                    dve.wait_ge(sem("probs_turned"), n4 + (b + 1))
                    V.tensor_copy(probsT[:, 4 * b:4 * b + 4, :], banks(b, 1, P)).then_inc(sem("probsT_odd"), 1)
                dve.wait_ge(sem("weighed"), n * 2)
                V.tensor_copy(outT[:, 4:HP, :], banks(5, 1, P)).then_inc(sem("outT_hi"), 1)

            link(normalize(xn[:], xt[:], 1), "x1_normed")
            normalize(xn2[:], xn[:], 2).then_inc(sem("xa_normed"), 1)
            dve.wait_ge(sem("mqa_keys_zero"), 1)
            dve.wait_ge(sem("mqa_kv_projected"), 1)
            V.tensor_copy(kT2[0:HD, 0:P], ps[0:HD, 2, 0:P])
            V.tensor_copy(kT2[HD:P, P:2 * P], ps[HD:P, 2, 0:P])
            V.tensor_copy(vmq[:], ps[:, 3, 0:HD]).then_inc(sem("mqa_kv_ready"), 1)
            attention(0, 1, negscale)
            dve.wait_ge(sem("attn_projected"), 1)
            link(normalize(onat, ps[:, 6, 0:D], 3), "ao_normed")
            link(V.tensor_tensor(onat, onat, rowv[:, LOG:LOG + D], ALU.mult), "ao_scaled")
            link(V.tensor_tensor(zb[:], xt[:], rowv[:, LOB:LOB + D], ALU.add), "xlb_ready")
            link(V.tensor_tensor(xt[:], zb[:], onat, ALU.add), "x2_ready")
            normalize(zt[:], xt[:], 4).then_inc(sem("z_ready"), 1)

            with dve.Fori(0, DEPTH) as i:
                dve.wait_ge(sem("layer_vectors_ready"), i + 1)
                for name, n in (("k", 1), ("q", 0)):
                    src = qkv_s[:, n * H:(n + 1) * H, :]
                    dst = rot[:, n * H:(n + 1) * H, :]
                    half = HD // 2
                    for k in range(2):
                        dve.wait_ge(sem(f"{name}_half_kept"), i * 2 + (k + 1))
                        hs = slice(k * HP, (k + 1) * HP)
                        V.tensor_tensor(dst[:, hs, :], src[:, hs, :], bg(rtab[:, 2 * n, :], HP, HD), ALU.mult)
                    V.tensor_tensor(swapped[:, :, 0:half], src[:, :, half:HD],
                                    bg(rtab[:, 2 * n + 1, 0:half], H, half), ALU.mult)
                    link(V.tensor_tensor(swapped[:, :, half:HD], src[:, :, 0:half],
                                         bg(rtab[:, 2 * n + 1, half:HD], H, half), ALU.mult),
                         f"{name}_steps", i * (3 + ROOT_STEPS) + 1)
                    added = V.tensor_tensor(dst, dst, swapped, ALU.add)
                    if name == "q":
                        added.then_inc(sem("q_rotated"), 1)
                    dve.wait_ge(sem(f"{name}_squared"), i + 1)
                    link(V.reduce_sum(nrm[:, n, :], squares[:, n * H:(n + 1) * H, :], AX_X), f"{name}_steps",
                         i * (3 + ROOT_STEPS) + 2)
                    link(V.tensor_scalar(nrm[:, n, :], nrm[:, n, :], NORM_FLOOR ** 2, None, ALU.max),
                         f"{name}_steps", i * (3 + ROOT_STEPS) + 3)
                    inverse_root(rnrm[:, n, :], nrm[:, n, :], newt[:, n, :], f"{name}_steps",
                                 i * (3 + ROOT_STEPS) + 3)
                    if name == "k":
                        V.tensor_tensor(dst, dst, bc(rnrm[:, n, :], H, HD), ALU.mult).then_inc(sem("k_rotated"), 1)
                V.tensor_scalar(expscale[:], rnrm[:, 0, :], QK_SCALE, None, ALU.mult)
                link(V.tensor_scalar(negscale[:], rnrm[:, 0, :], -QK_SCALE, None, ALU.mult), "scales_ready", i + 1)
                dve.wait_ge(sem("k_turned"), i + 1)
                V.tensor_copy(kT_s[HD:P, :, P:2 * P], banks(0, 2, P)[HD:P]).then_inc(sem("kT_hi"), 1)
                attention(i * 4 + 4, i + 2, negscale)
                dve.wait_ge(sem("attn_projected"), i + 2)
                V.tensor_tensor(zt[:], zt[:], ps[:, 6, 0:D], ALU.add).then_inc(sem("z_ready"), 1)
                dve.wait_ge(sem("z_ready"), i * 2 + 2)
                V.bn_stats(stats[:, 0, :], zt[:, 0:P])
                dve.wait_ge(sem("z_shifted"), i + 1)
                link(V.bn_stats(stats[:, 1, :], ps[:, 7, 0:P]), "f_steps", i * (3 + ROOT_STEPS) + 1)
                V.tensor_tensor(zb[:], zt[:], rowv[:, bass.ds(i * D + B2, D)], ALU.add).then_inc(sem("zb_ready"), 1)
                link(V.bn_aggr(mv[:], stats[:].rearrange("p a b -> p (a b)")), "f_steps",
                     i * (3 + ROOT_STEPS) + 2)
                link(V.tensor_scalar(mv[:, 1:2], mv[:, 1:2], EPS, None, ALU.add), "f_steps",
                     i * (3 + ROOT_STEPS) + 3)
                inverse_root(rstd[:], mv[:, 1:2], newt[:, 0, 0:1], "f_steps", i * (3 + ROOT_STEPS) + 3)
                V.tensor_scalar(xn2[:, 0:P], zt[:, 0:P], mv[:, 0:1], rstd[:, 0:1], ALU.subtract, ALU.mult)
                V.tensor_scalar(xn2[:, P:D], ps[:, 7, 0:P], mv[:, 0:1], rstd[:, 0:1], ALU.subtract, ALU.mult)\
                    .then_inc(sem("f_normed"), 1)
                dve.wait_ge(sem("lin_projected"), i + 1)
                for f in range(FB):
                    m = P if f < FB - 1 else FR
                    dve.wait_ge(sem("gelu_ready"), i * FB + (f + 1))
                    last = V.scalar_tensor_tensor(out=uT[0:m, f, :], in0=banks(1, 2, P)[0:m, f, :],
                                                  scalar=fcol[0:m, 2 * DB + f:2 * DB + f + 1], in1=gel[0:m, f, :],
                                                  op0=ALU.add, op1=ALU.mult)
                last.then_inc(sem("u_ready"), 1)
                dve.wait_ge(sem("zb_ready"), i + 1)
                dve.wait_ge(sem("ffn_projected"), i + 1)
                V.tensor_tensor(zt[:], zb[:], ps[:, 5, 0:D], ALU.add).then_inc(sem("z_ready"), 1)
            dve.wait_ge(sem("z_ready"), 2 * DEPTH + 1)
            V.tensor_tensor(xn[:], xt[:], zt[:], ALU.add).then_inc(sem("result"), 1)


_OUT = (P, D)


def kernel(**inputs):
    import numpy as _np
    import concourse.bacc as _bacc
    from concourse import mybir as _mybir
    from concourse.bass_utils import run_bass_kernel_spmd as _run

    a = {k: _np.asarray(v) for k, v in inputs.items()}

    def turn(w):
        return _np.ascontiguousarray(w.T)

    def cols(v, n):
        v = v.reshape(-1, v.shape[-1])
        full = _np.zeros((v.shape[0], n * P), v.dtype)
        full[:, :v.shape[1]] = v
        return full.reshape(v.shape[0] * n, P).T

    b1 = a["L0_ffn_b1"]
    colv = _np.ascontiguousarray(_np.concatenate([
        cols(a["L0_xattn_b_q"][ROW_FEATURE], DB), cols(a["L0_xattn_b_k"][ROW_FEATURE], DB), cols(a["L0_attn_ln_g"], DB),
        cols(a["L0_attn_ln_b"], DB), cols(a["L0_ffn_ln_g"], DB), cols(a["L0_ffn_ln_b"], DB),
        cols(b1[:, :FF], FB), cols(b1[:, FF:], FB)], axis=1))
    rowv = _np.concatenate([a[k].reshape(-1) for k in (
        "L0_xattn_b_v", "L0_xattn_b_o", "L0_attn_lno_g", "L0_attn_lno_b", "L0_ffn_b2",
        "L0_ffn_q_scale", "L0_ffn_k_scale")])
    arrays = {
        "x_in_dram": _np.ascontiguousarray(a["x"][0]),
        "ctxT_dram": turn(a["ctx_1024"][0]),
        "wqT_dram": turn(a["L0_xattn_W_q"][ROW_FEATURE]), "wkT_dram": turn(a["L0_xattn_W_k"][ROW_FEATURE]),
        "wvT_dram": turn(a["L0_xattn_W_v"]), "woT_dram": turn(a["L0_xattn_W_o"]),
        "aq_dram": turn(a["L0_attn_w_q"]), "akv_dram": turn(a["L0_attn_w_kv"]), "ao_dram": turn(a["L0_attn_w_out"]),
        "wqkv_dram": _np.ascontiguousarray(a["L0_ffn_Wqkv"]), "wo_dram": _np.ascontiguousarray(a["L0_ffn_Wo"]),
        "w1_dram": _np.ascontiguousarray(a["L0_ffn_W1"]), "w2_dram": _np.ascontiguousarray(a["L0_ffn_W2"]),
        "cols_dram": colv, "rows_dram": rowv, "consts_dram": constants(),
    }
    nc = _bacc.Bacc("TRN2", target_bir_lowering=False, num_devices=1)
    args = [nc.dram_tensor(n, v.shape, _mybir.dt.from_np(v.dtype), kind="ExternalInput").ap()
            for n, v in arrays.items()]
    args.append(nc.dram_tensor("out_dram", _OUT, _mybir.dt.float32, kind="ExternalOutput").ap())
    build(nc, *args)
    r = _run(nc, [arrays], core_ids=[0])
    return r.results[0]["out_dram"].reshape(1, P, D)
```

```python
from contextlib import ExitStack

import concourse.bass as bass
import numpy as np
from concourse import mybir

F32 = mybir.dt.float32
BF16 = mybir.dt.bfloat16
I32 = mybir.dt.int32
ALU = mybir.AluOpType
ACT = mybir.ActivationFunctionType
AX_X = mybir.AxisListType.X

P = 128
D = 256
DB = D // P
S = 12544
XH, XD = 16, 16
HT = P // XD
XS = float(XD) ** -0.5
C1 = 448
N1 = S // C1
C2 = 128
N2 = S // C2
UNIT = 2 * C2
NU = S // UNIT
KEY_PARTS = (0, 1, 2, 0, 1, 0)
QUERY_PARTS = (0, 0, 0, 1, 1, 2)
STACK = len(KEY_PARTS) * XD
COPIED = (0,2,3,4,6,7)
FOLDS = 4
SPREAD = 10
COPIES = 3
DIRECT = (1,5)
VW = XD + 1
H, HD = 16, 64
INNER = H * HD
HP = H // 2
FF = 682
FB = -(-FF // P)
FR = FF - (FB - 1) * P
DEPTH = 6
WINDOW = 64
MQA_SCALE = float(HD) ** -1.0
QK_SCALE = 8.0
EPS = 1e-5
MASKED = -1e30
NORM_FLOOR = 1e-12
NEWTON = 3
COLUMN_STEPS = 1 + 2 * NEWTON
WIDE_STEPS = 1 + 3 * NEWTON
BANK_ENDS = (3, FB - 1)
ROOT_GUESS = float(0x5F3759DF - (1 << 22) - (1 << 30))

HOLD_PROBS = (6, 3, 4, 4)
HOLD_SHIFT = 28
HOLD_ROTATE = 8
HOLD_NORM = 14

IDENT, SHIFT, HEADM, CAUSAL, BAND, COSQ, SINQ, COSK, SINK, CONSTS = np.cumsum(
    [0, P, P, HT, P, P, HD, HD, HD, HD]).tolist()
BQ, BK, LNG, LNB, FG, FBIAS, B1A, B1G, COLS = np.cumsum(
    [0, DB, DB, DB, DB, DB * DEPTH, DB * DEPTH, FB * DEPTH, FB * DEPTH]).tolist()
BV, BO, LOG, LOB, ROWX = np.cumsum([0, D, D, D, D]).tolist()
B2, QSC, KSC, ROWS = np.cumsum([0, D * DEPTH, HD * DEPTH, HD * DEPTH]).tolist()


ROW_FEATURE = np.arange(D).reshape(HT, DB, XD).transpose(1, 2, 0).reshape(D)


def constants():
    t = np.zeros((P, CONSTS), np.float32)
    i = np.arange(P)
    t[:, IDENT:IDENT + P] = np.eye(P)
    t[:, SHIFT:SHIFT + P] = np.eye(P, k=1)
    t[:, HEADM:HEADM + HT] = i[:, None] % HT == np.arange(HT)[None, :]
    q, k = i[:, None], i[None, :]
    t[:, CAUSAL:CAUSAL + P] = np.where(k > q, MASKED, 0.0)
    t[:, BAND:BAND + P] = np.where((k > q) | (q > k + WINDOW), MASKED, 0.0)
    half = np.arange(0, HD, 2, dtype=np.float32)
    freqs = i.astype(np.float32)[:, None] * (1.0 / 10000.0 ** (half / HD)).astype(np.float32)[None, :]
    base = (half + 0.4 * HD) / (1.4 * HD)
    power = (i - P // 2) / (WINDOW // 2)
    scale = (base[None, :].astype(np.float32) ** power[:, None].astype(np.float32)).astype(np.float32)
    cos, sin = np.cos(freqs), np.sin(freqs)
    for c0, s0, sc in ((COSQ, SINQ, scale), (COSK, SINK, 1.0 / scale)):
        t[:, c0:c0 + HD] = np.concatenate([cos * sc, cos * sc], 1)
        t[:, s0:s0 + HD] = np.concatenate([-sin * sc, sin * sc], 1)
    return t


def build(nc, x, ctxT, wqT, wkT, wvT, woT, aq, akv, ao, wqkv, wo, w1, w2, cols, rows, consts, out):
    with ExitStack() as ctx:
        def sb(name, shape, dt=F32):
            return ctx.enter_context(nc.sbuf_tensor(name, shape, dt))

        known = {}

        def sem(name):
            if name not in known:
                known[name] = ctx.enter_context(nc.semaphore(name))
            return known[name]

        ps = ctx.enter_context(nc.psum_tensor("ps", [P, 8, 512], F32))

        def banks(a, n, inner):
            return ps[:, a:a + n, :].rearrange("p b (g c) -> p (b g) c", c=inner)

        arena = sb("arena", [P, DB * S])
        keysT = arena[:].rearrange("p (t n) -> p t n", t=DB)
        place = [0]

        def view(n, c=None):
            v = arena[:, place[0]:place[0] + n]
            place[0] += n
            return v if c is None else v.rearrange("p (g c) -> p g c", c=c)

        wqkv_s = view(DB * 3 * INNER, 3 * INNER)
        wo_s = view(HP * D, D)
        w1_s = view(DB * 2 * FF, 2 * FF)
        w2_s = view(FB * D, D)
        qkv_s = view(3 * INNER, HD)
        rot = view(2 * INNER, HD)
        squares = view(2 * INNER, HD)
        aq_s = squares.rearrange("p g c -> p (g c)").rearrange("p (b n) -> p b n", b=DB)
        swapped = view(2 * INNER, HD)
        qT_s = view(HP * P, P)
        kT_s = view(HP * 2 * P, 2 * P)
        assert place[0] <= DB * S

        qbd16 = sb("qbd16", [P, DB, HT, P], BF16)
        keys16 = sb("keys16", [P, 2, DB, C1], BF16)
        ctx1 = sb("ctx1", [P, 2, DB, C1])
        ctx2 = sb("ctx2", [P, 2, DB, UNIT])
        qstack = sb("qstack", [P, XH, P], BF16)
        kstack = sb("kstack", [P, 2, XH, UNIT], BF16)
        queries = sb("queries", [P, DB, P])
        shift = sb("shift", [P, XH * P])
        expd = sb("expd", [P, 2, XH * P])
        vaug = sb("vaug", [P, 2, XH, VW])
        maxpart = sb("maxpart", [P, N1, XH])
        xmax = sb("xmax", [P, XH])
        wx = sb("wx", [P, 4, DB, D])
        akv_s = sb("akv_s", [P, DB, 2 * HD])
        ao_s = sb("ao_s", [P, HP, D])
        colv = sb("colv", [P, COLS])
        rowv = sb("rowv", [P, ROWS])
        con = sb("con", [P, CONSTS])
        ones16 = sb("ones16", [P, P], BF16)
        zeros16 = sb("zeros16", [P, P], BF16)
        xt = sb("xt", [P, D])
        zt = sb("zt", [P, D])
        xn = sb("xn", [P, D])
        xn2 = sb("xn2", [P, D])
        xT = sb("xT", [P, DB, P])
        kT2 = sb("kT2", [P, 2 * P])
        masks16 = sb("masks16", [P, 2, 4, P], BF16)
        ident16 = sb("ident16", [P, P], BF16)
        warm = sb("warm", [P, 2])
        expbias = sb("expbias", [P, H])
        expscale = sb("expscale", [P, H])
        negscale = sb("negscale", [P, H])
        vmq = sb("vmq", [P, HD])
        stats = sb("stats", [P, 2, 6])
        mv = sb("mv", [P, 2])
        rstd = sb("rstd", [P, 1])
        smax = sb("smax", [P, H])
        ssum = sb("ssum", [P, H])
        sinv = sb("sinv", [P, H])
        nrm = sb("nrm", [P, 2, H])
        rnrm = sb("rnrm", [P, 2, H])
        newt = sb("newt", [P, 2, H])
        rtab = sb("rtab", [P, 4, HD])
        zb = sb("zb", [P, D])
        oT_s = ctx1[:].rearrange("p a b n -> p (a b n)")[:, 0:512]
        fcol = sb("fcol", [P, 2 * DB + 2 * FB])
        onat = queries[:].rearrange("p b q -> p (b q)")
        probs = shift[:].rearrange("p (h q) -> p h q", q=P)
        uT = ctx1[:].rearrange("p a b n -> p (a b n)")[:, 512:512 + FB * P].rearrange("p (f q) -> p f q", q=P)
        kparts = ctx1[:].rearrange("p a b n -> p (a b n)").bitcast(BF16)[:, 0:2 * 3 * DB * UNIT].rearrange(
            "p (u s b n) -> p u s b n", u=2, s=3, b=DB)
        krest = keys16[:].rearrange("p a b n -> p (a b n)").bitcast(F32)[:, 0:DB * UNIT].rearrange(
            "p (b n) -> p b n", b=DB)
        flatstack = kstack[:].rearrange("p u g n -> p (u g n)")
        qparts = flatstack[:, 0:3 * DB * P].rearrange("p (s b q) -> p s b q", s=3, b=DB)
        rough = expd[:].rearrange("p a n -> p (a n)").bitcast(BF16)
        runmax = rough[:, 0:2 * len(COPIED) * C1].rearrange("p (a n) -> p a n", a=len(COPIED))
        spread = rough[:, 2 * len(COPIED) * C1:2 * len(COPIED) * C1 + XH * P].rearrange("p (h q) -> p h q", q=P)
        copied = rough[:, 2 * len(COPIED) * C1:2 * (len(COPIED) + COPIES) * C1].rearrange("p (a n) -> p a n", a=COPIES)
        probsT = expd[:, 0, :].rearrange("p (h q) -> p h q", q=P)
        outT = expd[:, 1, 0:HP * P].rearrange("p (h q) -> p h q", q=P)
        gel = expd[:, 1, HP * P:HP * P + FB * P].rearrange("p (f q) -> p f q", q=P)
        wq_s, wk_s, wv_s, wxo_s = (wx[:, n] for n in range(4))
        rowx = wx[:, 0:2].rearrange("p w b n -> p (w b n)")
        ident = con[:, IDENT:IDENT + P]
        shiftm = con[:, SHIFT:SHIFT + P]

        row_of = [h % DB * HT + h // DB for h in range(XH)]

        def blocks(w):
            return w.rearrange("(b p) n -> p b n", p=P)

        ctx_v = blocks(ctxT)

        def bc(v, g, c):
            return v.unsqueeze(2).to_broadcast([P, g, c])

        def bg(v, g, c):
            return v.unsqueeze(1).to_broadcast([P, g, c])

        def wait(eng, name, n):
            if not isinstance(n, int) or n > 0:
                eng.wait_ge(sem(name), n)

        def stacked(blk, part, dst):
            return (dst[XD * blk:XD * (blk + 1)].rearrange("d (j t) n -> d j (t n)", t=DB),
                    part.rearrange("p t n -> p (t n)"))

        block = ctx.enter_context(nc.Block())

        @block.sync
        def _(sp):
            def load(dst, src, name):
                sp.dma_start(dst, src).then_inc(sem(name), 16)

            load(xt[:], x, "x_in")
            load(con[:], consts, "con_in")
            load(colv[:], cols, "col_in")
            load(wq_s, blocks(wqT), "wq_in")
            load(wk_s, blocks(wkT), "wk_in")

            for c in range(2):
                load(ctx1[:, c], ctx_v[:, :, c * C1:(c + 1) * C1], f"ctx1_in{c}")
            def load_values(u, b):
                wait(sp, "values_projected", u * 2 - 2)
                load(ctx2[:, b], ctx_v[:, :, bass.ds(u * UNIT, UNIT)], f"ctx2_in{b}")

            def load_ctx(c, b):
                sp.wait_ge(sem("key_tiles_projected"), c * 2 - 2)
                load(ctx1[:, b], ctx_v[:, :, bass.ds(c * C1, C1)], f"ctx1_in{b}")

            load_ctx(2, 0)
            load_ctx(3, 1)
            sp.wait_ge(sem("queries_split"), 1)
            for blk, part in enumerate(QUERY_PARTS):
                load(*stacked(blk, qparts[:, part], qstack), "queries_stacked")
            with sp.Fori(2, N1 // 2) as i:
                for b in range(2):
                    load_ctx(i * 2 + b, b)
            load(wv_s, blocks(wvT), "wv_in")
            load_values(0, 0)
            load_values(1, 1)
            sp.wait_ge(sem("queries_stacked"), 16 * len(QUERY_PARTS))
            load(rowv[:], rows[ROWX:ROWX + ROWS].partition_broadcast(P), "row_in")
            sp.wait_ge(sem("key_tiles_projected"), N1 * DB)
            load(rowx, rows[0:ROWX].partition_broadcast(P), "row_in")
            load(wxo_s, blocks(woT), "wxo_in")
            load(akv_s[:], blocks(akv), "akv_in")
            load(ao_s[:], blocks(ao), "ao_in")

            def stack_keys(u, b):
                sp.wait_ge(sem("part3_ready"), u + 1)
                wait(sp, "scores_ready", u * 4 - 4)
                for blk, part in enumerate(KEY_PARTS):
                    load(*stacked(blk, kparts[:, b, part], kstack[:, b]), f"stacked{b}")

            stack_keys(0, 0)
            stack_keys(1, 1)
            with sp.Fori(1, NU // 2) as i:
                for b in range(2):
                    load_values(i * 2 + b, b)
                    stack_keys(i * 2 + b, b)
            load_values(NU - 1, 0)
            stack_keys(NU - 1, 0)

            def w2_loads(w2_i):
                load(w2_s[:, 0:FB - 1, :], w2_i[0:(FB - 1) * P, :].rearrange("(b p) n -> p b n", p=P), "w2_in")
                load(w2_s[0:FR, FB - 1, :], w2_i[(FB - 1) * P:FF, :], "w2_in")

            sp.wait_ge(sem("rest_ready"), NU)
            load(aq_s, blocks(aq), "aq_in")
            load(wqkv_s, blocks(wqkv[0]), "wqkv_in")
            load(wo_s, blocks(wo[0]), "wo_in")
            load(w1_s, blocks(w1[0]), "w1_in")
            w2_loads(w2[0])
            with sp.Fori(1, DEPTH) as i:
                sp.wait_ge(sem("v_projected"), i * 2)
                load(wqkv_s, blocks(wqkv[bass.ds(i, 1)].rearrange("a c n -> (a c) n")), "wqkv_in")
                sp.wait_ge(sem("attn_projected"), i + 1)
                load(wo_s, blocks(wo[bass.ds(i, 1)].rearrange("a c n -> (a c) n")), "wo_in")
                sp.wait_ge(sem("lin_projected"), i * 2)
                load(w1_s, blocks(w1[bass.ds(i, 1)].rearrange("a c n -> (a c) n")), "w1_in")
                sp.wait_ge(sem("ffn_projected"), i)
                w2_loads(w2[bass.ds(i, 1)].rearrange("a c n -> (a c) n"))
            sp.wait_ge(sem("result"), 1)
            load(out, xn[:], "stored")
            sp.wait_ge(sem("stored"), 16)

        @block.gpsimd
        def _(pool):
            nc.gpsimd.memset(runmax, -3e38).then_inc(sem("runmax_set"), 1)
            nc.gpsimd.memset(ones16[:], 1.0).then_inc(sem("ones_set"), 1)
            nc.gpsimd.memset(zeros16[:], 0.0).then_inc(sem("zeros_set"), 1)
            nc.gpsimd.memset(vaug[:], 1.0).then_inc(sem("vaug_set"), 1)

            nc.gpsimd.memset(kT2[:], 0.0).then_inc(sem("mqa_keys_zero"), 1)
            nc.gpsimd.memset(warm[:, 0:1], 0.0).then_inc(sem("gelu_warm"), 1)
            nc.gpsimd.memset(warm[:, 1:2], 0.0).then_inc(sem("exp_warm"), 1)
            pool.wait_ge(sem("con_in"), 16)
            nc.gpsimd.tensor_copy(ident16[:], ident)
            for m, c0 in enumerate((CAUSAL, BAND)):
                for k in range(4):
                    last = nc.gpsimd.tensor_copy(masks16[:, m, k, :], con[:, c0:c0 + P])
            last.then_inc(sem("masks_ready"), 1)

            def round_keys(c, b):
                pool.wait_ge(sem("tile0_kept"), c + 1)
                pool.wait_ge(sem("tile1_kept"), c + 1)
                wait(pool, "rough_for_copy", (c - 1) * len(COPIED))
                wait(pool, "rough_for_max", (c - 1) * len(DIRECT))
                nc.gpsimd.tensor_copy(keys16[:, b], keysT[:, :, bass.ds(c * C1, C1)]).then_inc(sem("keys_rounded"), 1)

            round_keys(0, 0)
            round_keys(1, 1)
            with pool.Fori(1, N1 // 2) as i:
                for b in range(2):
                    round_keys(i * 2 + b, b)

            def split_keys(u, b):
                pool.wait_ge(sem("part1_ready"), u + 1)
                wait(pool, "part3_ready", u)
                nc.gpsimd.tensor_tensor(krest, keysT[:, :, bass.ds(u * UNIT, UNIT)], kparts[:, b, 0], ALU.subtract)\
                    .then_inc(sem("rest_ready"), 1)
                pool.wait_ge(sem("part2_ready"), u + 1)
                nc.gpsimd.tensor_tensor(kparts[:, b, 2], krest, kparts[:, b, 1], ALU.subtract)\
                    .then_inc(sem("part3_ready"), 1)

            split_keys(0, 0)
            split_keys(1, 1)
            with pool.Fori(1, NU // 2) as i:
                for b in range(2):
                    split_keys(i * 2 + b, b)
            split_keys(NU - 1, 0)

            pool.wait_ge(sem("scores_ready"), 2 * N2)
            nc.gpsimd.memset(kT_s[:], 0.0).then_inc(sem("keys_zero"), 1)
            pool.wait_ge(sem("row_in"), 32)
            pool.wait_ge(sem("col_in"), 16)

            def layer_vectors(i):
                G = nc.gpsimd
                G.tensor_copy(fcol[:, 0:2 * DB].rearrange("p (b g) -> p g b", g=2),
                              colv[:, FG:B1A].rearrange("p (g l b) -> p g l b", g=2, b=DB)[:, :, bass.ds(i, 1), :]
                              .rearrange("p g l b -> p g (l b)"))
                G.tensor_copy(fcol[:, 2 * DB:].rearrange("p (g f) -> p g f", g=2),
                              colv[:, B1A:COLS].rearrange("p (g l f) -> p g l f", g=2, f=FB)[:, :, bass.ds(i, 1), :]
                              .rearrange("p g l f -> p g (l f)"))
                half = HD // 2
                for n, (r0, c0, s0) in enumerate(((QSC, COSQ, SINQ), (KSC, COSK, SINK))):
                    G.tensor_tensor(rtab[:, 2 * n, :], con[:, c0:c0 + HD], rowv[:, bass.ds(i * HD + r0, HD)], ALU.mult)
                    G.tensor_tensor(rtab[:, 2 * n + 1, 0:half], con[:, s0:s0 + half],
                                    rowv[:, bass.ds(i * HD + (r0 + half), half)], ALU.mult)
                    last = G.tensor_tensor(rtab[:, 2 * n + 1, half:HD], con[:, s0 + half:s0 + HD],
                                           rowv[:, bass.ds(i * HD + r0, half)], ALU.mult)
                last.then_inc(sem("layer_vectors_ready"), 1)

            layer_vectors(0)

            def prepare_rotation(i):
                half = HD // 2
                sq = squares[:, H:2 * H, :]
                pool.wait_ge(sem("k_squared"), i)
                nc.gpsimd.tensor_tensor(sq[:, :, 0:half], sq[:, :, 0:half], sq[:, :, half:HD], ALU.add)\
                    .then_inc(sem("k_folded"), 1)
                pool.wait_ge(sem("q_half_kept"), i * 2)
                pool.wait_ge(sem("layer_vectors_ready"), i)
                nc.gpsimd.tensor_tensor(swapped[:, 0:H, 0:half], qkv_s[:, 0:H, half:HD],
                                        bg(rtab[:, 1, 0:half], H, half), ALU.mult)
                nc.gpsimd.tensor_tensor(swapped[:, 0:H, half:HD], qkv_s[:, 0:H, 0:half],
                                        bg(rtab[:, 1, half:HD], H, half), ALU.mult).then_inc(sem("q_swapped"), 1)

            with pool.Fori(1, DEPTH) as i:
                prepare_rotation(i)
                pool.wait_ge(sem("u_ready"), i * FB)
                layer_vectors(i)
            prepare_rotation(DEPTH)

        @block.tensor
        def _(pe):
            mm = nc.tensor.matmul

            def project(dst, lhsT, rhs):
                for n, (a, b) in enumerate(zip(lhsT, rhs)):
                    last = mm(dst, a, b, start=n == 0, stop=n == len(lhsT) - 1)
                return last

            def transpose_blocks(dst, src, n=DB):
                for b in range(n):
                    last = nc.tensor.transpose(dst[:, b, :], src[:, b * P:(b + 1) * P], ident)
                return last

            pe.wait_ge(sem("con_in"), 16)
            pe.wait_ge(sem("xq_normed"), 1)
            transpose_blocks(banks(7, 1, P), xn).then_inc(sem("xq_turned"), 1)
            pe.wait_ge(sem("wq_in"), 16)
            pe.wait_ge(sem("xqT_ready"), 1)
            for t in range(DB):
                last = project(ps[:, 6, t * P:(t + 1) * P], [wq_s[:, b, t * P:(t + 1) * P] for b in range(DB)],
                               [xT[:, b, :] for b in range(DB)])
            last.then_inc(sem("queries_projected"), 1)

            def project_piece(b, n):
                t, k = divmod(n, DB)
                last = mm(ps[:, t, 0:C1], wk_s[:, k, t * P:(t + 1) * P], ctx1[:, b, k, :],
                          start=k == 0, stop=k == DB - 1)
                if k == DB - 1:
                    last.then_inc(sem("key_tiles_projected"), 1)

            def rough_scores(c, b, arrived=None):
                pe.wait_ge(sem("keys_rounded"), c + 1)
                for hp in range(XH // 2):
                    if hp in COPIED:
                        a = COPIED.index(hp)
                        b0 = 4 + 2 * (a % 2)
                        wait(pe, "rough_copied", c * len(COPIED) + (a - 1))
                        done = "rough_for_copy"
                    else:
                        b0 = 2
                        wait(pe, "maxima_taken", c * len(DIRECT) + DIRECT.index(hp))
                        done = "rough_for_max"
                    for k in range(2):
                        t, j = divmod(2 * hp + k, HT)
                        last = mm(ps[:, b0 + k, 0:C1], qbd16[:, t, j, :], keys16[:, b, t, :], start=True, stop=True)
                    last.then_inc(sem(done), 1)
                    if arrived is not None and hp % 2 == 0:
                        if hp == 0:
                            pe.wait_ge(sem(f"ctx1_in{b}"), arrived)
                        if hp % 4 == 0:
                            pe.wait_ge(sem(f"tile{hp // 4}_kept"), c + 2)
                        project_piece(b, hp // 2)

            pe.wait_ge(sem("wk_in"), 16)
            for b in range(2):
                pe.wait_ge(sem(f"ctx1_in{b}"), 16)
                for n in range(2 * DB):
                    if b and n % DB == 0:
                        pe.wait_ge(sem(f"tile{n // DB}_kept"), 1)
                    project_piece(b, n)
            pe.wait_ge(sem("queries_ready"), 1)
            rough_scores(0, 0, 32)
            rough_scores(1, 1, 32)
            with pe.Fori(1, N1 // 2 - 1) as i:
                rough_scores(i * 2, 0, i * 16 + 32)
                rough_scores(i * 2 + 1, 1, i * 16 + 32)
            rough_scores(N1 - 2, 0)
            rough_scores(N1 - 1, 1)

            def hold_clock(bank, n):
                for _ in range(n):
                    mm(ps[:, bank, :], ident16[:], masks16[:, 0].rearrange("p a b -> p (a b)"), start=True, stop=True)

            pe.wait_ge(sem("masks_ready"), 1)
            pe.wait_ge(sem("rough_copied"), N1 * len(COPIED))
            pe.wait_ge(sem("zeros_set"), 1)
            mm(ps[:, 4, :], zeros16[:], masks16[:, 0].rearrange("p a b -> p (a b)"), start=True, stop=False,
               skip_group_check=True)

            def values(c, j, arrived):
                b, ub = j % 2, j // 2
                pe.wait_ge(sem(f"ctx2_in{ub}"), arrived * 16)
                wait(pe, "values_kept", c - 1)
                cs = slice(b * C2, (b + 1) * C2)
                project(ps[:, 5 + b, 0:D], [ctx2[:, ub, k, cs] for k in range(DB)],
                        [wv_s[:, k, :] for k in range(DB)]).then_inc(sem("values_projected"), 1)

            pe.wait_ge(sem("wv_in"), 16)
            values(0, 0, 1)
            pe.wait_ge(sem("ones_set"), 1)
            hold_clock(7, HOLD_SHIFT)
            pe.wait_ge(sem("maxima_spread"), 2)
            for n in range(4):
                mm(ps[:, n, :], ones16[:], spread[:, 4 * n:4 * n + 4, :].rearrange("p a b -> p (a b)"),
                   start=True, stop=True).then_inc(sem("shift_summed"), 1)

            def scores(c, j, t):
                b, ub = j % 2, j // 2
                cs = slice(b * C2, (b + 1) * C2)
                wait(pe, "scores_shifted", c * 2 + (t - 1))
                for h in range(t * HT, (t + 1) * HT):
                    last = mm(banks(0, 4, P)[:, h, :], kstack[0:STACK, ub, h, cs], qstack[0:STACK, h, :],
                              start=True, stop=True)
                last.then_inc(sem("scores_ready"), 1)

            def weigh(c, b, t, last_step=False):
                if t == 0:
                    pe.wait_ge(sem("values_kept"), c + 1)
                pe.wait_ge(sem("exps_ready"), c * 2 + (t + 1))
                for h in range(t * HT, (t + 1) * HT):
                    g, j = divmod(h, 4)
                    last = mm(ps[32 * j:32 * j + VW, 4, g * P:(g + 1) * P], vaug[:, b, h, :],
                              expd[:, b, h * P:(h + 1) * P], start=False,
                              stop=last_step, skip_group_check=True)
                if t == DB - 1:
                    last.then_inc(sem("step_weighed"), 1)

            def products(c, j, arrived, first=False):
                pe.wait_ge(sem(f"stacked{j // 2}"), arrived * (16 * len(KEY_PARTS)))
                b1 = (j - 1) % 2
                scores(c, j, 0)
                if not first:
                    values(c, j, arrived)
                    weigh(c  - 1, b1, 0)
                scores(c, j, 1)
                if not first:
                    weigh(c  - 1, b1, 1)

            pe.wait_ge(sem("shift_ready"), 4)
            pe.wait_ge(sem("queries_stacked"), 16 * len(QUERY_PARTS))
            for c in range(4):
                products(c, c, 1, c == 0)
            with pe.Fori(1, N2 // 4) as i:
                for j in range(4):
                    products(i * 4 + j, j, i + 1)
            for c in (N2 - 2, N2 - 1):
                products(c, c % 4, N2 // 4 + 1)
            for t in range(DB):
                weigh(N2 - 1, 1, t, True)

            pe.wait_ge(sem("xout_kept"), 1)
            transpose_blocks(banks(0, 1, P), oT_s, 4).then_inc(sem("xout_turned"), 1)
            pe.wait_ge(sem("xout_normed"), 1)
            transpose_blocks(banks(1, 1, P), onat).then_inc(sem("xnat_turned"), 1)
            pe.wait_ge(sem("xnatT_ready"), 1)
            pe.wait_ge(sem("wxo_in"), 16)
            project(ps[:, 2, 0:D], [xT[:, b, :] for b in range(DB)],
                    [wxo_s[:, b, :] for b in range(DB)]).then_inc(sem("xattn_projected"), 1)

            def attention(n4, n, w, mask, qT, kT, v, pairs_kept=None):
                for b in range(4):
                    if pairs_kept is not None and b % 2 == 0:
                        pairs_kept(b // 2)
                    mm(ps[:, 4 + b, :], ident16[:], masks16[:, mask].rearrange("p a b -> p (a b)"),
                       start=True, stop=False)
                    for k in (2 * b, 2 * b + 1):
                        last = mm(banks(4, 4, 2 * P)[:, k, :], qT(k), kT(k), start=False, stop=k % 2 == 1)
                    last.then_inc(sem("sim_ready"), 1)
                for b in range(4):
                    hold_clock(b, HOLD_PROBS[b])
                    pe.wait_ge(sem("probs_ready"), n4 + (b + 1))
                    for h in range(4 * b, 4 * b + 4):
                        last = nc.tensor.transpose(banks(0, 4, P)[:, h, :], probs[:, h, :], ident)
                    last.then_inc(sem("probs_turned"), 1)
                for b in range(4):
                    if b % 2 == 0:
                        pe.wait_ge(sem("probsT_even"), n * 2 + (b // 2 - 1))
                    else:
                        pe.wait_ge(sem("probsT_odd"), n * 2 + (b // 2 - 1))
                    for h in range(4 * b, 4 * b + 4):
                        r = HD * (h % 2)
                        last = mm(banks(4, 2, P)[r:r + HD, h // 2, :], v(h), probsT[:, h, :], start=True, stop=True)
                    if b % 2:
                        last.then_inc(sem("weighed"), 1)
                pe.wait_ge(sem("outT_lo"), n)
                for k in range(HP):
                    if k == HP // 2:
                        pe.wait_ge(sem("outT_hi"), n)
                    last = mm(ps[:, 6, 0:D], outT[:, k, :], w[:, k, :], start=k == 0, stop=k == HP - 1)
                last.then_inc(sem("attn_projected"), 1)

            hold_clock(7, HOLD_NORM)
            pe.wait_ge(sem("xa_normed"), 1)
            transpose_blocks(banks(7, 1, P), xn2).then_inc(sem("xa_turned"), 1)
            pe.wait_ge(sem("xaT_ready"), 1)
            pe.wait_ge(sem("aq_in"), 16)
            pe.wait_ge(sem("akv_in"), 16)
            xTb = [xT[:, b, :] for b in range(DB)]
            for r in (0, HD):
                project(ps[r:r + HD, 2, 0:P], [akv_s[:, b, 0:HD] for b in range(DB)], xTb)
            project(ps[:, 3, 0:HD], xTb, [akv_s[:, b, HD:2 * HD] for b in range(DB)])\
                .then_inc(sem("mqa_kv_projected"), 1)
            for k in range(HP):
                last = project(banks(0, 2, P)[:, k, :], [aq_s[:, b, k * P:(k + 1) * P] for b in range(DB)], xTb)
            last.then_inc(sem("mqa_q_projected"), 1)
            pe.wait_ge(sem("mqa_kv_ready"), 1)
            pe.wait_ge(sem("mqa_q_ready"), 1)
            pe.wait_ge(sem("ao_in"), 16)
            pe.wait_ge(sem("masks_ready"), 1)
            attention(0, 1, ao_s, 0, lambda k: qT_s[:, k, :], lambda k: kT2[:], lambda h: vmq[:])

            hold_clock(0, 2 * HOLD_NORM)
            with pe.Fori(0, DEPTH) as i:
                pe.wait_ge(sem("z_ready"), i * 2 + 1)
                mm(ps[:, 0, 0:P], zt[:, 0:P], ident, start=True, stop=True)
                mm(ps[:, 0, P:2 * P], zt[:, P:2 * P], shiftm, start=True, stop=True)\
                    .then_inc(sem("z_turned"), 1)
                pe.wait_ge(sem("zT_ready"), i + 1)
                pe.wait_ge(sem("wqkv_in"), i * 16 + 16)
                for name, n in (("k", 1), ("q", 0), ("v", 2)):
                    for k in range(2):
                        c0 = n * INNER + k * 512
                        project(ps[:, 2 + 2 * n + k, :], xTb, [wqkv_s[:, b, c0:c0 + 512] for b in range(DB)])\
                            .then_inc(sem(f"{name}_projected"), 1)
                hold_clock(0, HOLD_ROTATE)
                for name, n, b0 in (("k", 1, 0), ("q", 0, 2)):
                    for half in range(2):
                        pe.wait_ge(sem(f"{name}_rotated"), i * 2 + (half + 1))
                        for k in range(half * HP // 2, (half + 1) * HP // 2):
                            src = rot[:, n * H + 2 * k:n * H + 2 * k + 2, :].rearrange("p a b -> p (a b)")
                            last = nc.tensor.transpose(banks(b0, 2, P)[:, k, :], src, ident)
                        last.then_inc(sem(f"{name}_turned"), 1)
                pe.wait_ge(sem("v_half_kept"), i * 2 + 2)

                def pairs_kept(half):
                    pe.wait_ge(sem("qT_ready"), i * 2 + (half + 1))
                    pe.wait_ge(sem("kT_lo"), i * 2 + (half + 1))
                    pe.wait_ge(sem("kT_hi"), i * 2 + (half + 1))

                pe.wait_ge(sem("wo_in"), i * 16 + 16)
                attention(i * 4 + 4, i + 2, wo_s, 1, lambda k: qT_s[:, k, :], lambda k: kT_s[:, k, :],
                          lambda h: qkv_s[:, 2 * H + h, :], pairs_kept)
                pe.wait_ge(sem("z_ready"), i * 2 + 2)
                mm(ps[:, 7, 0:P], shiftm, zt[:, P:2 * P], start=True, stop=True).then_inc(sem("z_shifted"), 1)
                hold_clock(0, HOLD_NORM)
                pe.wait_ge(sem("f_normed"), i + 1)
                transpose_blocks(banks(0, 1, P), xn2).then_inc(sem("f_turned"), 1)
                pe.wait_ge(sem("fT_ready"), i + 1)
                pe.wait_ge(sem("w1_in"), i * 16 + 16)
                rowsof = [P] * (FB - 1) + [FR]
                for g, b0, name in ((1, 3, "gate_projected"), (0, 1, "lin_projected")):
                    for f, m in enumerate(rowsof):
                        c0 = g * FF + f * P
                        last = project(banks(b0, 2, P)[0:m, f, :], [w1_s[:, b, c0:c0 + m] for b in range(DB)], xTb)
                        if f in BANK_ENDS:
                            last.then_inc(sem(name), 1)
                pe.wait_ge(sem("w2_in"), i * 32 + 32)
                for f, m in enumerate(rowsof):
                    pe.wait_ge(sem("u_ready"), i * FB + (f + 1))
                    last = mm(ps[:, 5, 0:D], uT[0:m, f, :], w2_s[0:m, f, :], start=f == 0, stop=f == FB - 1)
                last.then_inc(sem("ffn_projected"), 1)

        @block.scalar
        def _(act):
            def copy(dst, src):
                return nc.scalar.activation(dst, src, ACT.Copy)

            act.wait_ge(sem("xq_turned"), 1)
            copy(xT[:], banks(7, 1, P)[:, 0:DB, :]).then_inc(sem("xqT_ready"), 1)

            def keep_tile0(c):
                act.wait_ge(sem("key_tiles_projected"), c * 2 + 1)
                nc.scalar.activation(keysT[:, 0, bass.ds(c * C1, C1)], ps[:, 0, 0:C1], ACT.Identity,
                                     bias=colv[:, BK:BK + 1]).then_inc(sem("tile0_kept"), 1)

            def copy_rough(c, more=True):
                for a in range(len(COPIED)):
                    n = c * len(COPIED) + a
                    act.wait_ge(sem("rough_for_copy"), n + 1)
                    wait(act, "maxima_merged", n - (COPIES - 1))
                    copy(copied[:, a % COPIES].rearrange("p (k n) -> p k n", k=2),
                         ps[:, 4 + 2 * (a % 2):6 + 2 * (a % 2), 0:C1]).then_inc(sem("rough_copied"), 1)
                    if a == 2 and more:
                        keep_tile0(c + 2)

            act.wait_ge(sem("col_in"), 16)
            keep_tile0(0)
            keep_tile0(1)
            copy_rough(0)
            copy_rough(1)
            with act.Fori(1, N1 // 2 - 1) as i:
                for b in range(2):
                    copy_rough(i * 2 + b)
            copy_rough(N1 - 2, False)
            copy_rough(N1 - 1, False)

            def first_part(u, b):
                wait(act, f"stacked{b}", (u - b) * (8 * len(KEY_PARTS)))
                copy(kparts[:, b, 0], keysT[:, :, bass.ds(u * UNIT, UNIT)]).then_inc(sem("part1_ready"), 1)

            def second_part(u, b):
                act.wait_ge(sem("rest_ready"), u + 1)
                copy(kparts[:, b, 1], krest).then_inc(sem("part2_ready"), 1)

            for u in range(2):
                first_part(u, u)
                second_part(u, u)
            act.wait_ge(sem("xmax_ready"), 1)
            for h in range(SPREAD, XH):
                last = nc.scalar.activation(spread[:, h, :], ident16[:], ACT.Identity,
                                            scale=xmax[:, row_of[h]:row_of[h] + 1])
            last.then_inc(sem("maxima_spread"), 1)
            for n in (0, 1):
                act.wait_ge(sem("shift_summed"), n + 1)
                copy(shift[:, 512 * n:512 * (n + 1)], ps[:, n, :]).then_inc(sem("shift_ready"), 1)

            def exps(c, b, t):
                act.wait_ge(sem("scores_shifted"), c * 2 + (t + 1))
                half = expd[:, b, t * HT * P:(t + 1) * HT * P]
                nc.scalar.activation(half, half, ACT.Exp, scale=XS).then_inc(sem("exps_ready"), 1)

            def unit(u, b, ahead=True):
                exps(u * 2, 0, 0)
                if ahead:
                    first_part(u + 2, b)
                exps(u * 2, 0, 1)
                if ahead:
                    second_part(u + 2, b)
                exps(u * 2 + 1, 1, 0)
                exps(u * 2 + 1, 1, 1)

            with act.Fori(0, NU // 2 - 1) as i:
                for b in range(2):
                    unit(i * 2 + b, b)
            unit(NU - 3, 0)
            unit(NU - 2, 1, False)
            unit(NU - 1, 0, False)

            act.wait_ge(sem("step_weighed"), N2)
            copy(oT_s, ps[:, 4, :]).then_inc(sem("xout_kept"), 1)
            act.wait_ge(sem("xnat_turned"), 1)
            copy(xT[:], banks(1, 1, P)[:, 0:DB, :]).then_inc(sem("xnatT_ready"), 1)

            def attention(n4, n):
                for h in range(H):
                    if h % 4 == 0:
                        act.wait_ge(sem("bias_ready"), n4 + (h // 4 + 1))
                    last = nc.scalar.activation(probs[:, h, :], banks(4, 4, P)[:, h, :], ACT.Exp,
                                                scale=expscale[:, h:h + 1], bias=expbias[:, h:h + 1],
                                                accum_out=ssum[:, h:h + 1])
                    if h % 4 == 3:
                        last.then_inc(sem("sim_exp"), 1)

            def turned(n4, n):
                for b in (0, 2):
                    act.wait_ge(sem("probs_turned"), n4 + (b + 1))
                    copy(probsT[:, 4 * b:4 * b + 4, :], banks(b, 1, P)).then_inc(sem("probsT_even"), 1)
                act.wait_ge(sem("weighed"), n * 2 - 1)
                copy(outT[:, 0:4, :], banks(4, 1, P)).then_inc(sem("outT_lo"), 1)

            act.wait_ge(sem("xa_turned"), 1)
            for b in range(DB):
                last = nc.scalar.activation(xT[:, b, :], ps[:, 7, b * P:(b + 1) * P], ACT.Identity,
                                            scale=colv[:, LNG + b:LNG + b + 1], bias=colv[:, LNB + b:LNB + b + 1])
            last.then_inc(sem("xaT_ready"), 1)
            act.wait_ge(sem("mqa_q_projected"), 1)
            copy(qT_s, banks(0, 2, P)).then_inc(sem("mqa_q_ready"), 1)
            attention(0, 1)
            turned(0, 1)

            with act.Fori(0, DEPTH) as i:
                act.wait_ge(sem("z_turned"), i + 1)
                copy(xT[:], banks(0, 1, P)[:, 0:DB, :]).then_inc(sem("zT_ready"), 1)
                for name, n in (("k", 1), ("q", 0), ("v", 2)):
                    for k in range(2):
                        act.wait_ge(sem(f"{name}_projected"), i * 2 + (k + 1))
                        h0 = n * H + k * HP
                        copy(qkv_s[:, h0:h0 + HP, :], banks(2 + 2 * n + k, 1, HD)).then_inc(sem(f"{name}_half_kept"), 1)
                    if name == "v":
                        break
                    act.wait_ge(sem(f"{name}_half_kept"), i * 2 + 2)
                    nc.scalar.activation(squares[:, n * H:(n + 1) * H, :], qkv_s[:, n * H:(n + 1) * H, :], ACT.Square)\
                        .then_inc(sem(f"{name}_squared"), 1)
                for half in range(2):
                    act.wait_ge(sem("k_turned"), i * 2 + (half + 1))
                    copy(kT_s[0:HD, half * 4:half * 4 + 4, 0:P], banks(half, 1, P)[0:HD]).then_inc(sem("kT_lo"), 1)
                for half in range(2):
                    act.wait_ge(sem("q_turned"), i * 2 + (half + 1))
                    copy(qT_s[:, half * 4:half * 4 + 4, :], banks(2 + half, 1, P)).then_inc(sem("qT_ready"), 1)
                attention(i * 4 + 4, i + 2)
                turned(i * 4 + 4, i + 2)
                act.wait_ge(sem("gelu_warm"), i + 1)
                nc.scalar.activation(warm[:, 0:1], con[:, IDENT:IDENT + 1], ACT.Gelu).then_inc(sem("gelu_warm"), 1)
                act.wait_ge(sem("f_turned"), i + 1)
                for b in range(DB):
                    last = nc.scalar.activation(xT[:, b, :], ps[:, 0, b * P:(b + 1) * P], ACT.Identity,
                                                scale=fcol[:, 2 * b:2 * b + 1], bias=fcol[:, 2 * b + 1:2 * b + 2])
                last.then_inc(sem("fT_ready"), 1)
                for f in range(FB):
                    act.wait_ge(sem("gate_projected"), i * 2 + (f // 4 + 1))
                    m = P if f < FB - 1 else FR
                    nc.scalar.activation(gel[0:m, f, :], banks(3, 2, P)[0:m, f, :], ACT.Gelu,
                                         bias=fcol[0:m, 2 * DB + FB + f:2 * DB + FB + f + 1])\
                        .then_inc(sem("gelu_ready"), 1)
                act.wait_ge(sem("exp_warm"), i + 1)
                nc.scalar.activation(warm[:, 1:2], con[:, IDENT:IDENT + 1], ACT.Exp).then_inc(sem("exp_warm"), 1)

        @block.vector
        def _(dve):
            V = nc.vector

            def link(ins, name, n=1):
                ins.then_inc(sem(name), 1)
                dve.wait_ge(sem(name), n)

            def guess_root(y, w):
                return V.tensor_scalar(y.bitcast(I32), w.bitcast(I32), -0.5, ROOT_GUESS, ALU.mult, ALU.add)

            def column_root(y, w, a, name, n):
                link(guess_root(y, w), name, n + 1)
                for k in range(NEWTON):
                    link(V.scalar_tensor_tensor(out=a, in0=y, scalar=w, in1=y, op0=ALU.mult, op1=ALU.mult),
                         name, n + (2 * k + 2))
                    link(V.scalar_tensor_tensor(out=y, in0=a, scalar=1.5, in1=y, op0=ALU.add, op1=ALU.mult),
                         name, n + (2 * k + 3))

            def wide_root(y, w, a, name, n):
                link(guess_root(y, w), name, n + 1)
                for k in range(NEWTON):
                    link(V.tensor_tensor(a, y, y, ALU.mult), name, n + (3 * k + 2))
                    link(V.tensor_tensor(a, a, w, ALU.mult), name, n + (3 * k + 3))
                    link(V.scalar_tensor_tensor(out=y, in0=a, scalar=1.5, in1=y, op0=ALU.add, op1=ALU.mult),
                         name, n + (3 * k + 4))

            def half_variance(name, n, twice=False):
                scaled, added = (1.0 + EPS, EPS * EPS) if twice else (1.0, EPS)
                link(V.tensor_scalar(mv[:, 1:2], mv[:, 1:2], -0.5 * scaled, -0.5 * added, ALU.mult, ALU.add), name, n)

            def normalize(dst, src, run, twice=False):
                n = run * (3 + COLUMN_STEPS)
                link(V.bn_stats(stats[:, 0, :], src), "norm_steps", n + 1)
                link(V.bn_aggr(mv[:], stats[:, 0, :]), "norm_steps", n + 2)
                half_variance("norm_steps", n + 3, twice)
                column_root(rstd[:], mv[:, 1:2], newt[:, 0, 0:1], "norm_steps", n + 3)
                return V.tensor_scalar(dst, src, mv[:, 0:1], rstd[:, 0:1], ALU.subtract, ALU.mult)

            V.memset(expscale[:], MQA_SCALE)
            V.memset(negscale[:], -MQA_SCALE)
            dve.wait_ge(sem("x_in"), 16)
            normalize(xn[:], xt[:], 0).then_inc(sem("xq_normed"), 1)
            dve.wait_ge(sem("col_in"), 16)
            dve.wait_ge(sem("con_in"), 16)
            dve.wait_ge(sem("queries_projected"), 1)
            for t in range(DB):
                for j in range(HT):
                    V.tensor_scalar(qbd16[:, t, j, :], ps[:, 6, t * P:(t + 1) * P], colv[:, BQ + t:BQ + t + 1],
                                    con[:, HEADM + j:HEADM + j + 1], ALU.add, ALU.mult)
                last = V.tensor_scalar(queries[:, t, :], ps[:, 6, t * P:(t + 1) * P], colv[:, BQ + t:BQ + t + 1],
                                       None, ALU.add)
            last.then_inc(sem("queries_ready"), 1)

            def keep_tile1(c):
                dve.wait_ge(sem("key_tiles_projected"), c * 2 + 2)
                V.tensor_scalar(keysT[:, 1, bass.ds(c * C1, C1)], ps[:, 1, 0:C1], colv[:, BK + 1:BK + 2], None,
                                ALU.add).then_inc(sem("tile1_kept"), 1)

            def take_maxima(c, more=True):
                for hp in range(XH // 2):
                    if hp in COPIED:
                        a = COPIED.index(hp)
                        n = c * len(COPIED) + a
                        dve.wait_ge(sem("rough_copied"), n + 1)
                        V.tensor_tensor(runmax[:, a], runmax[:, a], copied[:, a % COPIES], ALU.max)\
                            .then_inc(sem("maxima_merged"), 1)
                    else:
                        dve.wait_ge(sem("rough_for_max"), c * len(DIRECT) + (DIRECT.index(hp) + 1))
                        V.reduce_max(maxpart[:, bass.ds(c, 1), 2 * hp:2 * hp + 2].rearrange("p c h -> p (c h)"),
                                     ps[:, 2:4, 0:C1], AX_X).then_inc(sem("maxima_taken"), 1)
                    if hp == 0 and more:
                        keep_tile1(c + 1)

            keep_tile1(0)
            dve.wait_ge(sem("queries_ready"), 1)
            for part in range(3):
                last = V.tensor_copy(qparts[:, part], queries[:])
                if part < 2:
                    link(last, "query_part", 2 * part + 1)
                    link(V.tensor_tensor(queries[:], queries[:], qparts[:, part], ALU.subtract),
                         "query_part", 2 * part + 2)
            last.then_inc(sem("queries_split"), 1)
            dve.wait_ge(sem("runmax_set"), 1)
            take_maxima(0)
            take_maxima(1)
            with dve.Fori(1, N1 // 2 - 1) as i:
                for b in range(2):
                    take_maxima(i * 2 + b)
            take_maxima(N1 - 2)
            take_maxima(N1 - 1, False)
            dve.wait_ge(sem("masks_ready"), 1)
            dve.wait_ge(sem("maxima_merged"), N1 * len(COPIED))
            rm = runmax.rearrange("p a (k n) -> p (a k) n", k=2)
            for fold in range(FOLDS):
                n = C1 >> (fold + 1)
                link(V.tensor_tensor(rm[:, :, 0:n], rm[:, :, 0:n], rm[:, :, n:2 * n], ALU.max), "folded", fold + 1)
            for a, hp in enumerate(COPIED):
                V.reduce_max(xmax[:, 2 * hp:2 * hp + 2], rm[:, 2 * a:2 * a + 2, 0:C1 >> FOLDS], AX_X)
            dve.wait_ge(sem("maxima_taken"), N1 * len(DIRECT))
            for hp in DIRECT:
                last = V.reduce_max(xmax[:, 2 * hp:2 * hp + 2],
                                    maxpart[:, :, 2 * hp:2 * hp + 2].rearrange("p c h -> p h c"), AX_X)
            link(last, "xmax_ready")
            for h in range(SPREAD):
                last = V.tensor_scalar(spread[:, h, :], ident16[:], xmax[:, row_of[h]:row_of[h] + 1], None, ALU.mult)
            last.then_inc(sem("maxima_spread"), 1)
            for n in (2, 3):
                dve.wait_ge(sem("shift_summed"), n + 1)
                V.tensor_copy(shift[:, 512 * n:512 * (n + 1)], ps[:, n, :]).then_inc(sem("shift_ready"), 1)
            dve.wait_ge(sem("vaug_set"), 1)
            dve.wait_ge(sem("shift_ready"), 4)

            def step(b, n, weighed=None):
                if weighed is not None:
                    dve.wait_ge(sem("step_weighed"), weighed)
                for t in range(DB):
                    dve.wait_ge(sem("scores_ready"), n + (t + 1))
                    cut = slice(t * HT * P, (t + 1) * HT * P)
                    V.tensor_tensor(expd[:, b, cut], ps[:, 2 * t:2 * t + 2, :].rearrange("p a b -> p (a b)"),
                                    shift[:, cut], ALU.subtract).then_inc(sem("scores_shifted"), 1)
                V.tensor_copy(vaug[:, b, :, 0:XD], ps[:, 5 + b, 0:D].rearrange("p (h d) -> p h d", d=XD))\
                    .then_inc(sem("values_kept"), 1)

            step(0, 0)
            step(1, 2)
            with dve.Fori(1, N2 // 2) as i:
                for b in range(2):
                    step(b, i * 4 + 2 * b, i * 2 + (b - 1))

            dve.wait_ge(sem("xout_turned"), 1)
            dve.wait_ge(sem("row_in"), 32)
            oview = ps[:, 0, :].rearrange("p (h c) -> p h c", c=32)
            link(V.reciprocal(sinv[:].unsqueeze(2), oview[:, :, XD:XD + 1]), "xsum_inverted")
            o3 = onat.rearrange("p (h d) -> p h d", d=XD)
            link(V.tensor_tensor(o3, oview[:, :, 0:XD], bc(sinv[:], XH, XD), ALU.mult), "xout_divided")
            V.tensor_tensor(onat, onat, rowx[:, BV:BV + D], ALU.add).then_inc(sem("xout_normed"), 1)
            link(V.tensor_tensor(zb[:], xt[:], rowx[:, BO:BO + D], ALU.add), "xb_ready")
            dve.wait_ge(sem("xattn_projected"), 1)
            link(V.tensor_tensor(xt[:], zb[:], ps[:, 2, 0:D], ALU.add), "x1_ready")

            def attention(n4, n, negscale):
                for b in range(4):
                    dve.wait_ge(sem("sim_ready"), n4 + (b + 1))
                    hs = slice(4 * b, 4 * b + 4)
                    link(V.reduce_max(smax[:, hs], banks(4 + b, 1, P), AX_X), "sim_max", n4 + (b + 1))
                    V.tensor_tensor(expbias[:, hs], smax[:, hs], negscale[:, hs], ALU.mult)\
                        .then_inc(sem("bias_ready"), 1)
                for b in range(4):
                    hs = slice(4 * b, 4 * b + 4)
                    dve.wait_ge(sem("sim_exp"), n4 + (b + 1))
                    link(V.reciprocal(sinv[:, hs], ssum[:, hs]), "sim_inverted", n4 + (b + 1))
                    V.tensor_tensor(probs[:, hs, :], probs[:, hs, :], bc(sinv[:, hs], 4, P), ALU.mult)\
                        .then_inc(sem("probs_ready"), 1)
                for b in (1, 3):
                    dve.wait_ge(sem("probs_turned"), n4 + (b + 1))
                    V.tensor_copy(probsT[:, 4 * b:4 * b + 4, :], banks(b, 1, P)).then_inc(sem("probsT_odd"), 1)
                dve.wait_ge(sem("weighed"), n * 2)
                V.tensor_copy(outT[:, 4:HP, :], banks(5, 1, P)).then_inc(sem("outT_hi"), 1)

            normalize(xn2[:], xt[:], 1, twice=True).then_inc(sem("xa_normed"), 1)
            dve.wait_ge(sem("mqa_keys_zero"), 1)
            dve.wait_ge(sem("mqa_kv_projected"), 1)
            V.tensor_copy(kT2[0:HD, 0:P], ps[0:HD, 2, 0:P])
            V.tensor_copy(kT2[HD:P, P:2 * P], ps[HD:P, 2, 0:P])
            V.tensor_copy(vmq[:], ps[:, 3, 0:HD]).then_inc(sem("mqa_kv_ready"), 1)
            attention(0, 1, negscale)
            dve.wait_ge(sem("attn_projected"), 1)
            link(normalize(onat, ps[:, 6, 0:D], 2), "ao_normed")
            link(V.tensor_tensor(onat, onat, rowx[:, LOG:LOG + D], ALU.mult), "ao_scaled")
            link(V.tensor_tensor(zb[:], xt[:], rowx[:, LOB:LOB + D], ALU.add), "xlb_ready")
            link(V.tensor_tensor(xt[:], zb[:], onat, ALU.add), "x2_ready")
            normalize(zt[:], xt[:], 3).then_inc(sem("z_ready"), 1)

            with dve.Fori(0, DEPTH) as i:
                dve.wait_ge(sem("layer_vectors_ready"), i + 1)
                half = HD // 2
                keys, queries_r = rot[:, H:2 * H, :], rot[:, 0:H, :]

                def scale_half(name, n, k):
                    dve.wait_ge(sem(f"{name}_half_kept"), i * 2 + (k + 1))
                    hs = slice(n * H + k * HP, n * H + (k + 1) * HP)
                    return V.tensor_tensor(rot[:, hs, :], qkv_s[:, hs, :], bg(rtab[:, 2 * n, :], HP, HD), ALU.mult)

                scale_half("k", 1, 0)
                scale_half("k", 1, 1)
                V.tensor_tensor(swapped[:, H:2 * H, 0:half], qkv_s[:, H:2 * H, half:HD],
                                bg(rtab[:, 3, 0:half], H, half), ALU.mult)
                step0 = i * (5 + WIDE_STEPS)
                link(V.tensor_tensor(swapped[:, H:2 * H, half:HD], qkv_s[:, H:2 * H, 0:half],
                                     bg(rtab[:, 3, half:HD], H, half), ALU.mult), "qk_steps", step0 + 1)
                V.tensor_tensor(keys, keys, swapped[:, H:2 * H, :], ALU.add).then_inc(sem("qk_steps"), 1)
                dve.wait_ge(sem("k_folded"), i + 1)
                V.reduce_sum(nrm[:, 1, :], squares[:, H:2 * H, 0:half], AX_X).then_inc(sem("qk_steps"), 1)
                scale_half("q", 0, 0)
                scale_half("q", 0, 1)
                dve.wait_ge(sem("q_squared"), i + 1)
                link(V.reduce_sum(nrm[:, 0, :], squares[:, 0:H, :], AX_X), "qk_steps", step0 + 4)
                link(V.tensor_scalar(nrm[:], nrm[:], NORM_FLOOR ** 2, -0.5, ALU.max, ALU.mult),
                     "qk_steps", step0 + 5)
                wide_root(rnrm[:], nrm[:], newt[:], "qk_steps", step0 + 5)
                for k in range(2):
                    hs = slice(k * HP, (k + 1) * HP)
                    V.tensor_tensor(keys[:, hs, :], keys[:, hs, :], bc(rnrm[:, 1, hs], HP, HD), ALU.mult)\
                        .then_inc(sem("k_rotated"), 1)
                dve.wait_ge(sem("q_swapped"), i + 1)
                for k in range(2):
                    hs = slice(k * HP, (k + 1) * HP)
                    V.tensor_tensor(queries_r[:, hs, :], queries_r[:, hs, :], swapped[:, hs, :], ALU.add)\
                        .then_inc(sem("q_rotated"), 1)
                for k in range(2):
                    dve.wait_ge(sem("k_turned"), i * 2 + (k + 1))
                    V.tensor_copy(kT_s[HD:P, k * 4:k * 4 + 4, P:2 * P], banks(k, 1, P)[HD:P])\
                        .then_inc(sem("kT_hi"), 1)
                V.tensor_scalar(expscale[:], rnrm[:, 0, :], QK_SCALE, None, ALU.mult)
                link(V.tensor_scalar(negscale[:], rnrm[:, 0, :], -QK_SCALE, None, ALU.mult), "scales_ready", i + 1)
                attention(i * 4 + 4, i + 2, negscale)
                dve.wait_ge(sem("attn_projected"), i + 2)
                V.tensor_tensor(zt[:], zt[:], ps[:, 6, 0:D], ALU.add).then_inc(sem("z_ready"), 1)
                dve.wait_ge(sem("z_ready"), i * 2 + 2)
                V.bn_stats(stats[:, 0, :], zt[:, 0:P])
                dve.wait_ge(sem("z_shifted"), i + 1)
                f_step = i * (3 + COLUMN_STEPS)
                link(V.bn_stats(stats[:, 1, :], ps[:, 7, 0:P]), "f_steps", f_step + 1)
                V.tensor_tensor(zb[:], zt[:], rowv[:, bass.ds(i * D + B2, D)], ALU.add).then_inc(sem("zb_ready"), 1)
                link(V.bn_aggr(mv[:], stats[:].rearrange("p a b -> p (a b)")), "f_steps", f_step + 2)
                half_variance("f_steps", f_step + 3)
                column_root(rstd[:], mv[:, 1:2], newt[:, 0, 0:1], "f_steps", f_step + 3)
                V.tensor_scalar(xn2[:, 0:P], zt[:, 0:P], mv[:, 0:1], rstd[:, 0:1], ALU.subtract, ALU.mult)
                V.tensor_scalar(xn2[:, P:D], ps[:, 7, 0:P], mv[:, 0:1], rstd[:, 0:1], ALU.subtract, ALU.mult)\
                    .then_inc(sem("f_normed"), 1)
                for f in range(FB):
                    m = P if f < FB - 1 else FR
                    dve.wait_ge(sem("lin_projected"), i * 2 + (f // 4 + 1))
                    dve.wait_ge(sem("gelu_ready"), i * FB + (f + 1))
                    V.scalar_tensor_tensor(out=uT[0:m, f, :], in0=banks(1, 2, P)[0:m, f, :],
                                           scalar=fcol[0:m, 2 * DB + f:2 * DB + f + 1], in1=gel[0:m, f, :],
                                           op0=ALU.add, op1=ALU.mult).then_inc(sem("u_ready"), 1)
                dve.wait_ge(sem("zb_ready"), i + 1)
                dve.wait_ge(sem("ffn_projected"), i + 1)
                V.tensor_tensor(zt[:], zb[:], ps[:, 5, 0:D], ALU.add).then_inc(sem("z_ready"), 1)
            dve.wait_ge(sem("z_ready"), 2 * DEPTH + 1)
            V.tensor_tensor(xn[:], xt[:], zt[:], ALU.add).then_inc(sem("result"), 1)


_OUT = (P, D)


def kernel(**inputs):
    import numpy as _np
    import concourse.bacc as _bacc
    from concourse import mybir as _mybir
    from concourse.bass_utils import run_bass_kernel_spmd as _run

    a = {k: _np.asarray(v) for k, v in inputs.items()}

    def turn(w):
        return _np.ascontiguousarray(w.T)

    def cols(v, n):
        v = v.reshape(-1, v.shape[-1])
        full = _np.zeros((v.shape[0], n * P), v.dtype)
        full[:, :v.shape[1]] = v
        return full.reshape(v.shape[0] * n, P).T

    b1 = a["L0_ffn_b1"]
    colv = _np.ascontiguousarray(_np.concatenate([
        cols(a["L0_xattn_b_q"][ROW_FEATURE], DB), cols(a["L0_xattn_b_k"][ROW_FEATURE], DB), cols(a["L0_attn_ln_g"], DB),
        cols(a["L0_attn_ln_b"], DB), cols(a["L0_ffn_ln_g"], DB), cols(a["L0_ffn_ln_b"], DB),
        cols(b1[:, :FF], FB), cols(b1[:, FF:], FB)], axis=1))
    rowv = _np.concatenate([a[k].reshape(-1) for k in (
        "L0_xattn_b_v", "L0_xattn_b_o", "L0_attn_lno_g", "L0_attn_lno_b", "L0_ffn_b2",
        "L0_ffn_q_scale", "L0_ffn_k_scale")])
    arrays = {
        "x_in_dram": _np.ascontiguousarray(a["x"][0]),
        "ctxT_dram": turn(a["ctx_1024"][0]),
        "wqT_dram": turn(a["L0_xattn_W_q"][ROW_FEATURE]), "wkT_dram": turn(a["L0_xattn_W_k"][ROW_FEATURE]),
        "wvT_dram": turn(a["L0_xattn_W_v"]), "woT_dram": turn(a["L0_xattn_W_o"]),
        "aq_dram": turn(a["L0_attn_w_q"]), "akv_dram": turn(a["L0_attn_w_kv"]), "ao_dram": turn(a["L0_attn_w_out"]),
        "wqkv_dram": _np.ascontiguousarray(a["L0_ffn_Wqkv"]), "wo_dram": _np.ascontiguousarray(a["L0_ffn_Wo"]),
        "w1_dram": _np.ascontiguousarray(a["L0_ffn_W1"]), "w2_dram": _np.ascontiguousarray(a["L0_ffn_W2"]),
        "cols_dram": colv, "rows_dram": rowv, "consts_dram": constants(),
    }
    nc = _bacc.Bacc("TRN2", target_bir_lowering=False, num_devices=1)
    args = [nc.dram_tensor(n, v.shape, _mybir.dt.from_np(v.dtype), kind="ExternalInput").ap()
            for n, v in arrays.items()]
    args.append(nc.dram_tensor("out_dram", _OUT, _mybir.dt.float32, kind="ExternalOutput").ap())
    build(nc, *args)
    r = _run(nc, [arrays], core_ids=[0])
    return r.results[0]["out_dram"].reshape(1, P, D)
```
